# Optimizing a Trainium2 kernel written in Bass

```python
import numpy as np
import jax
import jax.numpy as jnp

def _softmax(x, axis=-1):
    return jax.nn.softmax(x, axis=axis)

def _gelu(x):
    return jax.nn.gelu(x, approximate=True)

def _silu(x):
    return jax.nn.silu(x)

def _sigmoid(x):
    return jax.nn.sigmoid(x)

def _layernorm(x, axis=-1, eps=1e-05):
    m = jnp.mean(x, axis=axis, keepdims=True)
    v = jnp.var(x, axis=axis, keepdims=True)
    return (x - m) / jnp.sqrt(v + eps)

def _scatter_add(tgt, idx, src, axis=0):
    return tgt.at[idx].add(src)

def _segment_sum(src, seg, n):
    return jax.ops.segment_sum(src, seg, n)
kernel_name = 'mk_adj_preln_d4_adj_r2_33407f'

def setup_inputs(seed: int=0):
    np.random.seed(seed)
    _w = jnp.asarray

    def _rec_inputs():
        import jax
        import jax.numpy as jnp
        _gk = jax.random.key(seed)
        x = -9.806e-05 + 1 * jax.random.normal(jax.random.fold_in(_gk, 1), (2048, 64), jnp.float32)
        _a = jax.random.bernoulli(jax.random.fold_in(_gk, 2), 0.0078125, (2048, 2048))
        adj = _a.astype(jnp.int32)
        return (x, adj)
    x, adj = _rec_inputs()

    def _L0_gnn_setup():
        import jax, jax.numpy as jnp
        import numpy as np
        ALPHA = 0.2
        NEG_BIG = jnp.float32(-9000000000000000.0)
        key = jax.random.key(seed)
        k1, k2, k3, k4 = jax.random.split(key, 4)
        N, F_IN, F_OUT = (4096, 64, 64)
        inputs = jax.random.normal(k1, (N, F_IN), dtype=jnp.float32)
        adj = jax.random.randint(k2, (N, N), 0, 2, dtype=jnp.int32)
        gain = 1.414
        lim_w = gain * np.sqrt(6.0 / (F_IN + F_OUT))
        W = jax.random.uniform(k3, (F_IN, F_OUT), dtype=jnp.float32, minval=-lim_w, maxval=lim_w)
        lim_a = gain * np.sqrt(6.0 / (2 * F_OUT + 1))
        a = jax.random.uniform(k4, (2 * F_OUT, 1), dtype=jnp.float32, minval=-lim_a, maxval=lim_a)
        return {'inputs': inputs, 'adj': adj, 'W': W, 'a': a}
    _L0_gnn_all = _L0_gnn_setup()
    _L0_gnn_in = {k: v for k, v in _L0_gnn_all.items() if k in ('W', 'a')}
    del _L0_gnn_all

    def _L1_gnn_setup():
        import jax, jax.numpy as jnp
        import numpy as np
        ALPHA = 0.2
        NEG_INF = -9000000000000000.0
        key = jax.random.key(seed)
        k1, k2, k3, k4 = jax.random.split(key, 4)
        N, F_IN, F_OUT = (512, 64, 64)
        h = jax.random.normal(k1, (N, F_IN), dtype=jnp.float32)
        adj = jax.random.randint(k2, (N, N), 0, 2, dtype=jnp.int32)
        lim_W = 1.414 * np.sqrt(6.0 / (F_IN + F_OUT))
        W = jax.random.uniform(k3, (F_IN, F_OUT), minval=-lim_W, maxval=lim_W, dtype=jnp.float32)
        lim_a = 1.414 * np.sqrt(6.0 / (2 * F_OUT + 1))
        a = jax.random.uniform(k4, (2 * F_OUT, 1), minval=-lim_a, maxval=lim_a, dtype=jnp.float32)
        return {'h': h, 'adj': adj, 'W': W, 'a': a}
    _L1_gnn_all = _L1_gnn_setup()
    _L1_gnn_in = {k: v for k, v in _L1_gnn_all.items() if k in ('W', 'a')}
    del _L1_gnn_all

    def _L2_gnn_setup():
        import jax, jax.numpy as jnp
        import numpy as np
        N = 2048
        C = 64
        GDEP = 2
        HID = 32
        ALPHA = 0.2
        NEG_INF = jnp.float32(-9000000000000000.0)

        def _gat_layer(h, adj_mask, W_l, lw, lb, a):
            Wh = h @ W_l
            L1, L2 = (lw[:C], lw[C:])
            u = Wh @ L1 @ a
            v = Wh @ L2 @ a
            c = lb @ a
            e = jax.nn.leaky_relu(u + v.T + c, negative_slope=ALPHA)
            scores = jnp.where(adj_mask, e, NEG_INF)
            att = jax.nn.softmax(scores, axis=1)
            return jax.nn.elu(att @ Wh)
        key = jax.random.key(seed)
        ks = jax.random.split(key, 8)
        x = jax.random.normal(ks[0], (N, C), jnp.float32)
        adj = jax.random.randint(ks[1], (N, N), 0, 2, jnp.int32)
        W = jax.random.normal(ks[2], (GDEP, C, C), jnp.float32) / np.sqrt(C)
        lin_w = jax.random.normal(ks[3], (GDEP, 2 * C, HID), jnp.float32) / np.sqrt(2 * C)
        lin_b = jnp.zeros((GDEP, HID), jnp.float32)
        attn = jax.random.normal(ks[4], (GDEP, HID, 1), jnp.float32) / np.sqrt(HID)
        mlp_w = jax.random.normal(ks[5], ((GDEP + 1) * C, C), jnp.float32) / np.sqrt((GDEP + 1) * C)
        mlp_b = jnp.zeros((C,), jnp.float32)
        return dict(x=x, adj=adj, W=W, lin_w=lin_w, lin_b=lin_b, attn=attn, mlp_w=mlp_w, mlp_b=mlp_b)
    _L2_gnn_all = _L2_gnn_setup()
    _L2_gnn_in = {k: v for k, v in _L2_gnn_all.items() if k in ('W', 'lin_w', 'lin_b', 'attn', 'mlp_w', 'mlp_b')}
    del _L2_gnn_all

    def _L3_gnn_setup():
        import jax, jax.numpy as jnp
        import numpy as np
        N = 2048
        OUT = 64
        EMB = 8
        K_TAYLOR = 4
        EPS = 1e-12
        key = jax.random.key(seed)
        k1, k2, k3, k4 = jax.random.split(key, 4)
        h = jax.random.normal(k1, (N, OUT), dtype=jnp.float32)
        adj = jax.random.randint(k2, (N, N), 0, 2, dtype=jnp.int32)
        w_k = jax.random.normal(k3, (OUT, EMB), dtype=jnp.float32)
        w_q = jax.random.normal(k4, (OUT, EMB), dtype=jnp.float32)
        return {'h': h, 'adj': adj, 'w_k': w_k, 'w_q': w_q}
    _L3_gnn_all = _L3_gnn_setup()
    _L3_gnn_in = {k: v for k, v in _L3_gnn_all.items() if k in ('w_k', 'w_q')}
    del _L3_gnn_all
    return {'x': x, 'adj': adj, 'L0_gnn_W': _L0_gnn_in['W'], 'L0_gnn_a': _L0_gnn_in['a'], 'L1_gnn_W': _L1_gnn_in['W'], 'L1_gnn_a': _L1_gnn_in['a'], 'L2_gnn_W': _L2_gnn_in['W'], 'L2_gnn_lin_w': _L2_gnn_in['lin_w'], 'L2_gnn_lin_b': _L2_gnn_in['lin_b'], 'L2_gnn_attn': _L2_gnn_in['attn'], 'L2_gnn_mlp_w': _L2_gnn_in['mlp_w'], 'L2_gnn_mlp_b': _L2_gnn_in['mlp_b'], 'L3_gnn_w_k': _L3_gnn_in['w_k'], 'L3_gnn_w_q': _L3_gnn_in['w_q']}

def reference(x, adj, L0_gnn_W, L0_gnn_a, L1_gnn_W, L1_gnn_a, L2_gnn_W, L2_gnn_lin_w, L2_gnn_lin_b, L2_gnn_attn, L2_gnn_mlp_w, L2_gnn_mlp_b, L3_gnn_w_k, L3_gnn_w_q):
    import jax
    import jax.numpy as jnp

    def _L0_gnn_ref(inputs, adj, W, a):
        import jax, jax.numpy as jnp
        import numpy as np
        ALPHA = 0.2
        NEG_BIG = jnp.float32(-9000000000000000.0)
        Wh = inputs @ W
        F_out = W.shape[1]
        a_src = a[:F_out, 0]
        a_dst = a[F_out:, 0]
        e = (Wh @ a_src)[:, None] + (Wh @ a_dst)[None, :]
        e = jnp.where(e > 0, e, ALPHA * e)
        scores = jnp.where(adj > 0, e, NEG_BIG)
        attention = jax.nn.softmax(scores, axis=1)
        h_prime = attention @ Wh
        return jax.nn.elu(h_prime)

    def _L1_gnn_ref(h, adj, W, a):
        import jax, jax.numpy as jnp
        import numpy as np
        ALPHA = 0.2
        NEG_INF = -9000000000000000.0
        F_OUT = W.shape[1]
        Wh = h @ W
        a1, a2 = (a[:F_OUT, 0], a[F_OUT:, 0])
        e = (Wh @ a1)[:, None] + (Wh @ a2)[None, :]
        e = jax.nn.leaky_relu(e, negative_slope=ALPHA)
        scores = jnp.where(adj > 0, e, jnp.float32(NEG_INF))
        attention = jax.nn.softmax(scores, axis=1)
        h_prime = attention @ Wh
        return jax.nn.elu(h_prime)

    def _L2_gnn_ref(x, adj, W, lin_w, lin_b, attn, mlp_w, mlp_b):
        import jax, jax.numpy as jnp
        import numpy as np
        N = 2048
        C = 64
        GDEP = 2
        HID = 32
        ALPHA = 0.2
        NEG_INF = jnp.float32(-9000000000000000.0)

        def _gat_layer(h, adj_mask, W_l, lw, lb, a):
            Wh = h @ W_l
            L1, L2 = (lw[:C], lw[C:])
            u = Wh @ L1 @ a
            v = Wh @ L2 @ a
            c = lb @ a
            e = jax.nn.leaky_relu(u + v.T + c, negative_slope=ALPHA)
            scores = jnp.where(adj_mask, e, NEG_INF)
            att = jax.nn.softmax(scores, axis=1)
            return jax.nn.elu(att @ Wh)
        mask = adj > 0
        h = x
        outs = [h]
        for i in range(GDEP):
            h = ALPHA * x + (1.0 - ALPHA) * _gat_layer(h, mask, W[i], lin_w[i], lin_b[i], attn[i])
            outs.append(h)
        ho = jnp.concatenate(outs, axis=-1)
        return ho @ mlp_w + mlp_b

    def _L3_gnn_ref(h, adj, w_k, w_q):
        import jax, jax.numpy as jnp
        import numpy as np
        N = 2048
        OUT = 64
        EMB = 8
        K_TAYLOR = 4
        EPS = 1e-12
        h = h - h.mean(axis=-1, keepdims=True)
        h = h / jnp.maximum(jnp.linalg.norm(h, axis=-1, keepdims=True), EPS)
        k = h @ w_k
        q = h @ w_q
        scores = k @ q.T / jnp.sqrt(jnp.float32(EMB))
        a_att = jax.nn.softmax(scores, axis=-1)
        a = adj.astype(jnp.float32) * a_att
        a = a / a.sum(axis=-1, keepdims=True)
        result = a
        fact = 1.0
        for i in range(2, K_TAYLOR):
            a = a @ a
            fact = fact * i
            result = result + a / fact
        return result @ h
    h = jnp.maximum(_layernorm(x, axis=-1), 0.0)
    x = x + _L0_gnn_ref(h, adj, L0_gnn_W, L0_gnn_a)
    h = jnp.maximum(_layernorm(x, axis=-1), 0.0)
    x = x + _L1_gnn_ref(h, adj, L1_gnn_W, L1_gnn_a)
    h = jnp.maximum(_layernorm(x, axis=-1), 0.0)
    x = x + _L2_gnn_ref(h, adj, L2_gnn_W, L2_gnn_lin_w, L2_gnn_lin_b, L2_gnn_attn, L2_gnn_mlp_w, L2_gnn_mlp_b)
    h = jnp.maximum(_layernorm(x, axis=-1), 0.0)
    x = x + _L3_gnn_ref(h, adj, L3_gnn_w_k, L3_gnn_w_q)
    return x

_drawn_inputs = setup_inputs


def setup_inputs(seed=0):
    import zlib

    import numpy as np

    out = dict(_drawn_inputs(seed))
    spreads = {'L2_gnn_lin_b': (0.0, 0.8), 'L2_gnn_mlp_b': (0.0, 0.1)}
    factors = {'L2_gnn_lin_w': 5.053, 'L2_gnn_attn': 5.097, 'L3_gnn_w_k': 4.288, 'L3_gnn_w_q': 3.666}
    for name, (base, spread) in spreads.items():
        noise = np.random.default_rng([zlib.crc32(name.encode()), seed]).standard_normal(out[name].shape)
        drawn = base * np.exp(spread * noise) if base else spread * noise
        out[name] = jnp.asarray(drawn.astype(out[name].dtype))
    for name, factor in factors.items():
        out[name] = (out[name] * factor).astype(out[name].dtype)
    return out
```

```python
import math
from contextlib import ExitStack

import concourse.bass as bass
from concourse import mybir


P = 128
N = 2048
F = 64
NB = N // P
CH = 1024
NCH = N // CH
CB = CH // P
BANK = 512
U = 4
GAT = 4
EMB = 8
BIG = 2.0 ** 100
SLOPE = 0.2
PARTS = 3
KR = PARTS * PARTS * EMB
HS = 64.0
PS = 12 * math.log(2.0)
TB = 3


def program(nc, x_d, adjT_d, w_d, a01_d, lwT_d, lb_d, at_d, mw_d, mb_d, wkq_d, id_d, out_d):
    f32, bf16, f16, i32 = mybir.dt.float32, mybir.dt.bfloat16, mybir.dt.float16, mybir.dt.int32
    ALU, ACT, AX = mybir.AluOpType, mybir.ActivationFunctionType, mybir.AxisListType
    ctx = ExitStack()
    with ctx:
        def sb(name, shape, dt):
            return ctx.enter_context(nc.sbuf_tensor(name, shape, dt))

        def ps(name, shape):
            return ctx.enter_context(nc.psum_tensor(name, shape, f32))

        def sem(name):
            return ctx.enter_context(nc.semaphore(name))

        nadj = sb("nadj", [P, NB, N], bf16)
        phi = nadj[:].bitcast(f16)
        big = sb("big", [P, NB * N], bf16)
        plo = big[:].bitcast(f16).rearrange("p (b n) -> p b n", b=NB)
        stage = big[:, 0:4 * 2 * N].bitcast(i32).rearrange("p (s n) -> p s n", s=4)
        cand = big[:, 8 * N:8 * N + U * N].rearrange("p (u n) -> p u n", u=U)
        tmp = big[:, 12 * N:14 * N].bitcast(f32).rearrange("p (u n) -> p u n", u=2)
        prob = sb("prob", [P, U, CH], f32)
        e32 = prob
        accm = sb("accm", [P, N], bf16)
        accf = big[:, 8 * N:10 * N].bitcast(f32)
        wB = sb("wB", [P, N], f32)
        KT = sb("KT", [KR + PARTS, N], bf16)
        QT = sb("QT", [KR + PARTS, N], bf16)
        rowW = KT[0:PARTS, :]
        rowA = QT[0:PARTS, :]
        ident = sb("ident", [P, P], f32)
        identb = sb("identb", [P, P], bf16)
        bigI = sb("bigI", [P, P], bf16)
        fold = sb("fold", [P, F], f32)
        ones3 = sb("ones3", [PARTS, P], bf16)
        x = sb("x", [P, NB, F], f32)
        h0 = sb("h0", [P, NB, F], f32)
        h1 = sb("h1", [P, NB, F], f32)
        hT = [sb(f"hT{k}", [P, NB // 2 * P], f32) for k in range(3)]
        WhA = sb("WhA", [P, NB, F + 1], f32)
        wt = sb("wt", [P, GAT, F + 2], f32)
        wTt = sb("wTt", [F, GAT, P], f32)
        av = sb("av", [F, GAT, 2], f32)
        lwT = sb("lwT", [32, 2, P], f32)
        atv = sb("atv", [32, 2], f32)
        lbv = sb("lbv", [32, 2], f32)
        cb = sb("cb", [P, 2], f32)
        mw = sb("mw", [P, 3, F], f32)
        mb = sb("mb", [P, F], f32)
        wkq = sb("wkq", [P, 2 * EMB], f32)
        uv = sb("uv", [P, NB, 2], f32)
        uc = sb("uc", [P, NB], f32)
        wc = sb("wc", [P, NB], f32)
        r1 = sb("r1", [P, NB], f32)
        r2 = sb("r2", [P, NB], f32)
        v8 = sb("v8", [P, NB], f32)
        v2 = sb("v2", [P, NB], f32)
        vc = sb("vc", [P, NB], f32)
        vm = sb("vm", [P, NB], f32)
        mc = sb("mc", [P, NB], f32)
        ac = sb("ac", [P, NB], f32)
        w3 = sb("w3", [P, NB, PARTS], bf16)
        a3 = sb("a3", [P, NB, PARTS], bf16)
        rec = sb("rec", [P, NB], f32)
        o = sb("o", [P, CB, F], f32)
        g = sb("g", [P, CB, F], f32)
        s1 = sb("s1", [P, CB], f32)
        var = sb("var", [P, CB], f32)
        rstd = sb("rstd", [P, CB], f32)
        mhalf = sb("mhalf", [P, CB], f32)
        pbias = sb("pbias", [P, 1], f32)
        seed = sb("seed", [P, 5], f32)
        kq = sb("kq", [P, NB, 2 * EMB], f32)
        kqr = sb("kqr", [P, NB, 2 * EMB], f32)
        Kst = accm[:, 0:NB * (KR + PARTS)].rearrange("p (b r) -> p b r", b=NB)
        Qst = hT[2][:].bitcast(bf16)[:, 0:NB * (KR + PARTS)].rearrange("p (b r) -> p b r", b=NB)
        HY = [t.bitcast(f16)[:, 0:NB * (2 * F + 1)].rearrange("p (b f) -> p b f", b=NB)
              for t in (wB[:, 0:NB * (F + 1)], WhA[:].rearrange("p b f -> p (b f)"))]
        y = hT[1][:].rearrange("p (b f) -> p b f", f=F)
        res = h1
        Tsb = prob[:, 0:2, :].rearrange("p u n -> p (u n)")

        X = [ps(f"X{k}", [P, CH]) for k in range(2)]
        ACC = ps("ACC", [P, 3 * BANK])
        MISC = ps("MISC", [P, BANK])
        Rb = ACC[:, 0:2 * BANK].bitcast(bf16)
        Xb = [t[:].bitcast(bf16) for t in X]

        def wh_view(par):
            return X[par][:].rearrange("p (k n) -> p k n", k=2)[:, :, 0:4 * (F + 2)] \
                .rearrange("p k (s f) -> p k s f", f=F + 2)

        ld_w = sem("ld_w")
        ld_adj = [sem(f"ld_adj{k}") for k in range(4)]
        st_out = sem("st_out")
        adj_ready = sem("adj_ready")
        consts = sem("consts")
        dve_const = sem("dve_const")
        dve_step = sem("dve_step")
        pe_prep = sem("pe_prep")
        prep_ready = sem("prep_ready")
        h_ready = sem("h_ready")
        hT_psum = sem("hT_psum")
        hT_ready = sem("hT_ready")
        wh_psum = sem("wh_psum")
        v_ready = sem("v_ready")
        wh_ready = sem("wh_ready")
        w3_ready = sem("w3_ready")
        wrow_psum = sem("wrow_psum")
        wrow_ready = sem("wrow_ready")
        wB_psum = sem("wB_psum")
        wB_ready = sem("wB_ready")
        cand_ready = [sem(f"cand_ready{k}") for k in range(U)]
        max_done = sem("max_done")
        accm_clear = sem("accm_clear")
        maxT_psum = sem("maxT_psum")
        a3_ready = sem("a3_ready")
        arow_psum = sem("arow_psum")
        arow_ready = sem("arow_ready")
        x_ready = sem("x_ready")
        tmp_ready = sem("tmp_ready")
        p_ready = sem("p_ready")
        lo_ready = sem("lo_ready")
        p_free = sem("p_free")
        neg_ready = sem("neg_ready")
        eo_ready = sem("eo_ready")
        acc_free = sem("acc_free")
        var_ready = sem("var_ready")
        rstd_ready = sem("rstd_ready")
        mlp_psum = sem("mlp_psum")
        kq_psum = sem("kq_psum")
        kq_ready = sem("kq_ready")
        kqT_psum = sem("kqT_psum")
        kqT_ready = sem("kqT_ready")
        t_ready = sem("t_ready")
        t_sb = sem("t_sb")
        f_ready = sem("f_ready")
        y_ready = sem("y_ready")
        out_ready = sem("out_ready")

        block = ctx.enter_context(nc.Block())

        N_C = 4
        N_W = 20

        @block.sync
        def _(sp):
            xv = x_d.rearrange("(b p) f -> p b f", p=P)
            sp.dma_start(x[:], xv).then_inc(ld_w, 16)
            sp.dma_start(ident[:], id_d).then_inc(ld_w, 16)
            for half in range(2):
                lo = half * F
                sp.dma_start(wt[lo:lo + F, :, 0:F], w_d[0].rearrange("l k f -> k l f")).then_inc(ld_w, 16)
                sp.dma_start(wTt[:, :, lo:lo + F], w_d[1].rearrange("l k f -> k l f")).then_inc(ld_w, 16)
                sp.dma_start(mw[lo:lo + F, :, :], mw_d.rearrange("(t c) f -> c t f", c=F)).then_inc(ld_w, 16)
                sp.dma_start(wkq[lo:lo + F, 0:EMB], wkq_d[0]).then_inc(ld_w, 16)
                sp.dma_start(wkq[lo:lo + F, EMB:2 * EMB], wkq_d[1]).then_inc(ld_w, 16)
                sp.dma_start(fold[lo:lo + F, :], id_d[0:F, 0:F]).then_inc(ld_w, 16)
            sp.dma_start(lwT[:], lwT_d.rearrange("l h c -> h l c")).then_inc(ld_w, 16)
            sp.dma_start(atv[:], at_d).then_inc(ld_w, 16)
            sp.dma_start(lbv[:], lb_d).then_inc(ld_w, 16)
            sp.dma_start(mb[:], mb_d.broadcast_to([P, F])).then_inc(ld_w, 16)
            for l in range(2):
                sp.dma_start(av[:, l, :], a01_d[l]).then_inc(ld_w, 16)
            for s in range(4):
                sp.dma_start(stage[:, s, :], adjT_d[s * P:(s + 1) * P, :]).then_inc(ld_adj[s], 16)
            with sp.Fori(4, NB - 3, 4) as i:
                for s in range(4):
                    sp.wait_ge(adj_ready, i + (s - 3))
                    sp.dma_start(stage[:, s, :],
                                 adjT_d[bass.ds((i + s) * P, P), :]).then_inc(ld_adj[s], 16)
            ov = out_d.rearrange("(b p) f -> p b f", p=P)
            for c in range(4):
                sp.wait_ge(out_ready, c + 1)
                sp.dma_start(ov[:, 4 * c:4 * c + 4, :], x[:, 4 * c:4 * c + 4, :]).then_inc(st_out, 16)
            sp.wait_ge(st_out, 64)

        @block.gpsimd
        def _(pool):
            pool.memset(ones3[:], 1.0).then_inc(consts, 1)
            pool.memset(pbias[:], PS).then_inc(consts, 1)
            pool.memset(WhA[:, :, F:F + 1], 1.0).then_inc(consts, 1)
            pool.memset(mhalf[:], -0.5).then_inc(consts, 1)
            n_rstd = [0]

            def inverse_root():
                n_rstd[0] += 1
                pool.wait_ge(var_ready, n_rstd[0])
                pool.tensor_tensor(rstd[:], var[:], mhalf[:], ALU.pow).then_inc(rstd_ready, 1)

            for c in range(NCH):
                if c == 0:
                    pool.wait_ge(consts, N_C)
                inverse_root()
            for l in range(GAT):
                if l:
                    pool.wait_ge(maxT_psum, l)
                pool.memset(accm[:], -BIG).then_inc(accm_clear, 1)
                pool.wait_ge(v_ready, l + 1)
                for jb in range(U - 1, NB, U):
                    if l == 0:
                        pool.wait_ge(adj_ready, jb + 1)
                    pool.wait_ge(max_done, NB * l + jb + 1)
                    pool.tensor_scalar(cand[:, U - 1, :], nadj[:, jb, :], BIG, vc[:, jb:jb + 1],
                                       ALU.mult, ALU.add).then_inc(cand_ready[U - 1], U)
                if l in (0, 1):
                    for c in range(NCH):
                        inverse_root()
            for c in range(2 * NCH):
                inverse_root()

        @block.scalar
        def _(act):
            act.wait_ge(consts, N_C)
            for l in range(GAT):
                slot = (0, 0, 0, 1)[l]
                act.wait_ge(hT_psum, l + 1)
                act.activation(hT[slot][:], X[0][:], ACT.Copy).then_inc(hT_ready, 1)
                act.wait_ge(v_ready, l + 1)
                for par in range(2):
                    act.activation(WhA[:, par::2, 0:F].rearrange("p (k s) f -> p k s f", k=2),
                                   wh_view(par)[:, :, :, 0:F], ACT.Copy).then_inc(wh_ready, 1)
                act.wait_ge(wrow_psum, l + 1)
                act.activation(rowW, Rb[0:PARTS, :], ACT.Copy).then_inc(wrow_ready, 1)
                with act.Fori(0, NB - U + 1, U) as i:
                    for k in range(2):
                        if l == 0:
                            act.wait_ge(adj_ready, i + (k + 1))
                        act.wait_ge(max_done, i + (NB * l + k + 1))
                        act.activation(cand[:, k, :], nadj[:, bass.ds(i + k, 1), :].rearrange("p a n -> p (a n)"),
                                       ACT.Identity, bias=vc[:, bass.ds(i + k, 1)],
                                       scale=BIG).then_inc(cand_ready[k], U)
                for k in range(2):
                    act.wait_ge(wB_psum, 2 * l + k + 1)
                    act.activation(wB[:, k * CH:(k + 1) * CH], X[k][:], ACT.Copy).then_inc(wB_ready, 1)
                act.wait_ge(arow_psum, l + 1)
                act.activation(rowA, Rb[0:PARTS, :], ACT.Copy).then_inc(arow_ready, 1)
                for c in range(NCH):
                    t0 = NB * (NCH * l + c)
                    with act.Fori(0, NB - U + 1, U) as i:
                        for k in range(U):
                            act.wait_ge(tmp_ready, i + (t0 + k + 3))
                            act.wait_ge(p_free, i + (t0 + k + 1))
                            act.activation(prob[:, k, :], tmp[:, k % 2, :], ACT.Exp,
                                           bias=v2[:, bass.ds(i + k, 1)]).then_inc(p_ready, 1)
                    act.wait_ge(neg_ready, NCH * l + c + 1)
                    act.activation(g[:], g[:], ACT.Exp).then_inc(eo_ready, 1)
                if l == GAT - 1:
                    act.wait_ge(hT_psum, GAT + 1)
                    act.activation(hT[2][:], X[0][:], ACT.Copy).then_inc(hT_ready, 1)
            act.wait_ge(hT_psum, GAT + 2)
            act.activation(hT[0][:], X[0][:], ACT.Copy).then_inc(hT_ready, 1)
            act.wait_ge(kqT_psum, 1)
            act.activation(KT[:], Xb[0][0:KR + PARTS, :], ACT.Copy)
            act.activation(QT[:], Xb[1][0:KR + PARTS, :], ACT.Copy).then_inc(kqT_ready, 1)
            act.wait_ge(kqT_psum, 2)
            act.activation(KT[:], Xb[0][0:KR + PARTS, :], ACT.Copy).then_inc(kqT_ready, 1)
            tg = GAT * NCH * NB
            tm = NCH * NB
            for c in range(NCH):
                with act.Fori(0, NB - U + 1, U) as i:
                    for k in range(U):
                        t = tg + NB * c + k
                        act.wait_ge(x_ready, i + (tm + t + 1))
                        act.wait_ge(lo_ready, i + (NB * c + k + 1))
                        act.activation(e32[:, k, :], X[k % 2][:], ACT.Exp, bias=pbias[:, 0:1])
                        act.activation(phi[:, bass.ds(i + k, 1), c * CH:(c + 1) * CH]
                                       .rearrange("p a n -> p (a n)"),
                                       X[k % 2][:], ACT.Exp, bias=pbias[:, 0:1]).then_inc(p_ready, 1)
            for q in range(3):
                for ic in range(4):
                    act.wait_ge(t_ready, 4 * q + ic + 1)
                    act.activation(Tsb[:, ic * BANK:(ic + 1) * BANK],
                                   X[ic // 2][:, (ic % 2) * BANK:(ic % 2 + 1) * BANK],
                                   ACT.Copy).then_inc(t_sb, 1)

        @block.tensor
        def _(pe):
            def transpose_h(src, chunks, prior):
                for k in range(NB // 2):
                    if k % 4 == 0:
                        pe.wait_ge(h_ready, prior + k // 4 + 1)
                    last = pe.transpose(X[0][:, k * P:(k + 1) * P],
                                        src[:, 2 * k:2 * k + 2, :].rearrange("p a f -> p (a f)"), ident[:])
                last.then_inc(hT_psum, 1)

            def lhs(t, b):
                return t[F * (b % 2):F * (b % 2) + F, (b // 2) * P:(b // 2 + 1) * P]

            def half(t, b):
                return t[F * (b % 2):F * (b % 2) + F]

            pe.wait_ge(ld_w, 16 * N_W)
            for l in range(2):
                for t in range(2):
                    pe.matmul(MISC[0:F, 2 * l + t:2 * l + t + 1], lwT[:, l, t * F:(t + 1) * F],
                              atv[:, l:l + 1], start=True, stop=True)
                last = pe.matmul(MISC[:, 8 + l:9 + l], lbv[:, l:l + 1].broadcast_to([32, P]), atv[:, l:l + 1],
                                 start=True, stop=True)
            last.then_inc(pe_prep, 1)
            pe.wait_ge(prep_ready, 1)
            for l in range(GAT):
                last = pe.matmul(MISC[:, 16 + 2 * l:18 + 2 * l], wTt[:, l, :], av[:, l, :], start=True, stop=True)
            last.then_inc(pe_prep, 1)
            pe.wait_ge(prep_ready, 2)
            pe.wait_ge(dve_const, 2)

            def mask_tile(n, c, jb, row):
                buf = X[n % 2]
                pe.wait_ge(row["free"], row["count"])
                for s in range(2):
                    pe.matmul(buf[:, s * BANK:(s + 1) * BANK], bigI[:],
                              row["mask"][:, s * BANK:(s + 1) * BANK], start=True, stop=False)
                for s in range(2):
                    last = pe.matmul(buf[:, s * BANK:(s + 1) * BANK], row["lhs"],
                                     row["rhs"][:, s * BANK:(s + 1) * BANK], start=False, stop=True)
                last.then_inc(x_ready, 1)

            def mask_at(c, jb):
                return nadj[:, bass.ds(jb, 1), c * CH:(c + 1) * CH].rearrange("p a n -> p (a n)")

            def score_gat(l, c, jb, k):
                mask_tile(k, c, jb, {"free": tmp_ready, "count": jb + (NB * (NCH * l + c) + 1), "mask": mask_at(c, jb),
                                     "lhs": ones3[:], "rhs": rowA[:, c * CH:(c + 1) * CH]})

            def products_gat(l, c, jb, k, first, last_tile):
                pe.wait_ge(p_ready, jb + (NB * (NCH * l + c) + 3))
                rhs = WhA[:, bass.ds(jb, 1), :].rearrange("p a n -> p (a n)")
                for b in range(CB):
                    at = (b // 4) * BANK + (b % 4) * (F + 1)
                    last = pe.matmul(ACC[:, at:at + F + 1], prob[:, k, b * P:(b + 1) * P], rhs,
                                     start=first and b % 4 == 0, stop=last_tile, skip_group_check=True)
                last.then_inc(p_free, 1)

            for l in range(GAT):
                slot = (0, 0, 0, 1)[l]
                transpose_h((h0, h0, h0, h1)[l], NCH, NCH * l)
                pe.wait_ge(hT_ready, l + 1)
                for b in range(NB):
                    at = (b // 8) * BANK + (b // 2 % 4) * (F + 2)
                    last = pe.matmul(X[b % 2][:, at:at + F + 2], lhs(hT[slot], b), half(wt, b)[:, l, :],
                                     start=True, stop=True)
                last.then_inc(wh_psum, 1)
                pe.wait_ge(w3_ready, l + 1)
                for b in range(NB):
                    last = pe.transpose(Rb[0:PARTS, b * P:(b + 1) * P], w3[:, b, :], identb[:])
                last.then_inc(wrow_psum, 1)
                pe.wait_ge(wrow_ready, l + 1)
                pe.wait_ge(wh_ready, 2 * l + 2)
                for k in range(2):
                    for s in range(2):
                        at = k * CH + s * BANK
                        last = pe.matmul(X[k][:, s * BANK:(s + 1) * BANK], ones3[:], rowW[:, at:at + BANK],
                                         start=True, stop=True)
                    last.then_inc(wB_psum, 1)
                pe.wait_ge(wB_ready, 2 * l + 2)
                pe.wait_ge(max_done, U + NB * (l + 1))
                for b in range(NB):
                    last = pe.transpose(Xb[0][:, b * P:(b + 1) * P], accm[:, b * P:(b + 1) * P], identb[:])
                last.then_inc(maxT_psum, 1)
                pe.wait_ge(a3_ready, l + 1)
                for b in range(NB):
                    last = pe.transpose(Rb[0:PARTS, b * P:(b + 1) * P], a3[:, b, :], identb[:])
                last.then_inc(arow_psum, 1)
                pe.wait_ge(arow_ready, l + 1)
                for c in range(NCH):
                    score_gat(l, c, 0, 0)
                    score_gat(l, c, 1, 1)
                    if l or c:
                        pe.wait_ge(acc_free, NCH * l + c)
                    for k in range(2):
                        products_gat(l, c, k, k, k == 0, False)
                        score_gat(l, c, k + 2, k)
                    with pe.Fori(2, NB - 1 - U, U) as i:
                        for k in range(U):
                            products_gat(l, c, i + k, (k + 2) % U, False, False)
                            score_gat(l, c, i + (k + 2), k)
                    for k in range(2, 4):
                        products_gat(l, c, NB - 4 + k, k, False, True)

            transpose_h(h1, NCH, NCH * GAT)
            pe.wait_ge(hT_ready, GAT + 1)
            pe.wait_ge(acc_free, NCH * GAT)
            for b in range(NB):
                out = X[b % 2][:, (b // 2) * F:(b // 2 + 1) * F]
                for t in range(3):
                    last = pe.matmul(out, lhs(hT[t], b), half(mw, b)[:, t, :], start=t == 0, stop=t == 2)
            last.then_inc(mlp_psum, 1)

            transpose_h(h0, NCH, NCH * (GAT + 1))
            pe.wait_ge(hT_ready, GAT + 2)
            for b in range(NB):
                last = pe.matmul((MISC, ACC)[b % 2][:, (b // 2) * 2 * EMB:(b // 2 + 1) * 2 * EMB], lhs(hT[0], b), half(wkq, b),
                                 start=True, stop=True)
            last.then_inc(kq_psum, 1)
            pe.wait_ge(kq_ready, 1)
            for b in range(NB):
                pe.transpose(Xb[0][0:KR + PARTS, b * P:(b + 1) * P], Kst[:, b, :], identb[:])
                last = pe.transpose(Xb[1][0:KR + PARTS, b * P:(b + 1) * P], Qst[:, b, :], identb[:])
            last.then_inc(kqT_psum, 1)
            pe.wait_ge(kqT_ready, 1)

            def score_taylor(rows, free, n0, c, jb, k):
                mask_tile(k, c, jb, {"free": free, "count": jb + n0, "mask": mask_at(c, jb),
                                     "lhs": QT[0:rows, bass.ds(jb * P, P)],
                                     "rhs": KT[0:rows, c * CH:(c + 1) * CH]})

            for c in range(NCH):
                with pe.Fori(0, NB - U + 1, U) as i:
                    for k in range(U):
                        score_taylor(KR, max_done, U + NB * (GAT + c) - 1, c, i + k, k)
            pe.wait_ge(max_done, U + NB * GAT + NCH * NB)
            for b in range(NB):
                last = pe.transpose(X[b // CB][:, (b % CB) * P:(b % CB + 1) * P], accf[:, b * P:(b + 1) * P], ident[:])
            last.then_inc(maxT_psum, 1)
            pe.wait_ge(kq_ready, 2)
            for b in range(NB):
                last = pe.transpose(Xb[0][0:KR + PARTS, b * P:(b + 1) * P], Kst[:, b, :], identb[:])
            last.then_inc(kqT_psum, 1)
            pe.wait_ge(kqT_ready, 2)

            def products_taylor(c, jb, k, first, last_tile):
                n = GAT * NCH * NB + NB * c
                pe.wait_ge(p_ready, jb + (n + 3))
                pe.wait_ge(lo_ready, jb + (U + NB * c + 1))
                rhs = HY[0][:, bass.ds(jb, 1), :].rearrange("p a n -> p (a n)")
                for b in range(CB):
                    at = (b // TB) * BANK + (b % TB) * (2 * F + 1)
                    cols = slice(c * CH + b * P, c * CH + (b + 1) * P)
                    for part in (phi, plo):
                        last = pe.matmul(ACC[:, at:at + 2 * F + 1],
                                         part[:, bass.ds(jb, 1), cols].rearrange("p a n -> p (a n)"), rhs,
                                         start=first and b % TB == 0 and part is phi, stop=last_tile and part is plo,
                                         skip_group_check=True)
                last.then_inc(p_free, 1)

            for c in range(NCH):
                n0 = NB * (NCH * GAT + c) + 1
                score_taylor(KR + PARTS, p_ready, n0, c, 0, 0)
                score_taylor(KR + PARTS, p_ready, n0, c, 1, 1)
                if c:
                    pe.wait_ge(acc_free, NCH * GAT + 1 + c)
                else:
                    pe.wait_ge(acc_free, NCH * GAT + 1)
                for k in range(2):
                    products_taylor(c, k, k, k == 0, False)
                    score_taylor(KR + PARTS, p_ready, n0, c, k + 2, k)
                with pe.Fori(2, NB - 1 - U, U) as i:
                    for k in range(U):
                        products_taylor(c, i + k, (k + 2) % U, False, False)
                        score_taylor(KR + PARTS, p_ready, n0, c, i + (k + 2), k)
                for k in range(2, 4):
                    products_taylor(c, NB - 4 + k, k, False, True)

            def turn_back(q, ic):
                pe.wait_ge(t_sb, 4 * q + ic + 1)
                before = 4 * q + ic - 2
                if before < 8:
                    pe.wait_ge(y_ready, NCH + max(before + 1, 0))
                else:
                    pe.wait_ge(out_ready, before - 7)
                for b in range(4):
                    last = pe.matmul(ACC[:, (ic % 2) * BANK + b * F:(ic % 2) * BANK + (b + 1) * F],
                                     Tsb[:, ic * BANK + b * P:ic * BANK + (b + 1) * P], fold[:],
                                     start=True, stop=True)
                last.then_inc(f_ready, 1)

            for q in range(3):
                for ic in range(4):
                    out = X[ic // 2][:, (ic % 2) * BANK:(ic % 2 + 1) * BANK]
                    if q:
                        pe.wait_ge(t_sb, 4 * (q - 1) + ic + 1)
                    cols = slice(ic * BANK, (ic + 1) * BANK)

                    def pair(jb, first, final):
                        lhsT = HY[(q + 1) % 2][:, bass.ds(jb, 1), 0:2 * F].rearrange("p a n -> p (a n)")
                        pe.matmul(out, lhsT, phi[:, bass.ds(jb, 1), cols].rearrange("p a n -> p (a n)"),
                                  start=first, stop=False)
                        return pe.matmul(out, lhsT, plo[:, bass.ds(jb, 1), cols].rearrange("p a n -> p (a n)"),
                                         start=False, stop=final)

                    for jb4 in range(4):
                        if ic == 0:
                            pe.wait_ge(y_ready, (NCH * (jb4 // 2) // 2 + 1) if q == 0 else NCH + 4 * (q - 1) + jb4 + 1)
                        if jb4 == 0:
                            pair(0, True, False)
                            with pe.Fori(1, 4) as i:
                                pair(i, False, False)
                        elif jb4 < 3:
                            with pe.Fori(4 * jb4, 4 * jb4 + 4) as i:
                                pair(i, False, False)
                        else:
                            with pe.Fori(12, NB - 1) as i:
                                pair(i, False, False)
                            if ic:
                                turn_back(q, ic - 1)
                            pair(NB - 1, False, True).then_inc(t_ready, 1)
                turn_back(q, 3)

        @block.vector
        def _(dve):
            steps = [0]

            def link(ins):
                steps[0] += 1
                ins.then_inc(dve_step, 1)
                dve.wait_ge(dve_step, steps[0])

            def signal(ins, s, value):
                ins.then_inc(s, 1)
                dve.wait_ge(s, value)

            def bcast(t, n=F):
                return t.unsqueeze(2).broadcast_to([P, t.shape[1], n])

            n_rstd = [0]

            def normalise(src, dst, relu, var_scale, eps, mode, scratch):
                link(dve.tensor_reduce(s1[:], src, AX.X, ALU.add))
                link(dve.tensor_scalar(s1[:], s1[:], 1.0 / F, None, ALU.mult))
                link(dve.tensor_tensor(scratch, src, bcast(s1[:]), ALU.subtract))
                link(dve.tensor_tensor(o[:], scratch, scratch, ALU.mult))
                link(dve.tensor_reduce(s1[:], o[:], AX.X, ALU.add))
                dve.tensor_scalar(var[:], s1[:], var_scale, eps, ALU.mult, mode).then_inc(var_ready, 1)
                n_rstd[0] += 1
                dve.wait_ge(rstd_ready, n_rstd[0])
                if relu:
                    return dve.scalar_tensor_tensor(dst, scratch, 0.0, bcast(rstd[:]), ALU.max, ALU.mult)
                return dve.tensor_tensor(dst, scratch, bcast(rstd[:]), ALU.mult)

            def layernorm(c):
                b = slice(CB * c, CB * (c + 1))
                return normalise(x[:, b, :], h0[:, b, :], True, 1.0 / F, 1e-5, ALU.add, g[:])

            def split(src, dst, n):
                link(dve.tensor_copy(dst[0], src))
                link(dve.tensor_tensor(r1[:, 0:n], src, dst[0], ALU.subtract))
                link(dve.tensor_copy(dst[1], r1[:, 0:n]))
                link(dve.tensor_tensor(r2[:, 0:n], r1[:, 0:n], dst[1], ALU.subtract))
                return dve.tensor_copy(dst[2], r2[:, 0:n])

            dve.wait_ge(ld_w, 16 * N_W)
            dve.wait_ge(consts, N_C)
            for n, (start, count) in enumerate([(tmp_ready, 2), (p_ready, 2), (max_done, U), (p_free, U), (lo_ready, U)]):
                dve.memset(seed[:, n:n + 1], 0.0).then_inc(start, count)
            dve.tensor_copy(identb[:], ident[:]).then_inc(dve_const, 1)
            dve.tensor_scalar(bigI[:], ident[:], BIG, None, ALU.mult).then_inc(dve_const, 1)
            dve.wait_ge(pe_prep, 1)
            dve.tensor_copy(cb[:], MISC[:, 8:10])
            dve.tensor_copy(av[:, 2:4, :], MISC[0:F, 0:4].rearrange("p (l t) -> p l t", l=2)).then_inc(prep_ready, 1)
            for c in range(NCH):
                layernorm(c).then_inc(h_ready, 1)
                dve.wait_ge(h_ready, c + 1)
            dve.wait_ge(pe_prep, 2)
            dve.tensor_copy(wt[:, :, F:F + 2],
                            MISC[:, 16:16 + 2 * GAT].rearrange("p (l t) -> p l t", l=GAT)).then_inc(prep_ready, 1)

            for l in range(GAT):
                dve.wait_ge(wh_psum, l + 1)
                for par in range(2):
                    ins = dve.tensor_copy(uv[:, par::2, :].rearrange("p (k s) t -> p k s t", k=2),
                                          wh_view(par)[:, :, :, F:F + 2])
                link(ins)
                dve.tensor_copy(vc[:], uv[:, :, 1]).then_inc(v_ready, 1)
                dve.tensor_scalar(v8[:], uv[:, :, 1], 1 - SLOPE, None, ALU.mult)
                dve.tensor_scalar(v2[:], uv[:, :, 1], SLOPE, None, ALU.mult)
                if l >= 2:
                    link(dve.tensor_scalar(uc[:], uv[:, :, 0], cb[:, l - 2:l - 1], None, ALU.add))
                else:
                    link(dve.tensor_copy(uc[:], uv[:, :, 0]))
                link(dve.tensor_scalar(wc[:], uc[:], -(1 - SLOPE), None, ALU.mult))
                signal(split(wc[:], [w3[:, :, k] for k in range(PARTS)], NB), w3_ready, l + 1)
                dve.wait_ge(accm_clear, l + 1)
                with dve.Fori(0, NB - U + 1, U) as i:
                    if l == 0:
                        for k in range(U):
                            dve.wait_ge(ld_adj[k], i * 4 + 16)
                            dve.tensor_scalar(nadj[:, bass.ds(i + k, 1), :].rearrange("p a n -> p (a n)"),
                                              stage[:, k, :], 0, -1.0, ALU.is_gt, ALU.add).then_inc(adj_ready, 1)
                        dve.wait_ge(adj_ready, i + U)
                    dve.wait_ge(max_done, i + (NB * l + 3))
                    dve.tensor_scalar(cand[:, 2, :], nadj[:, bass.ds(i + 2, 1), :].rearrange("p a n -> p (a n)"),
                                      BIG, vc[:, bass.ds(i + 2, 1)], ALU.mult, ALU.add).then_inc(cand_ready[2], U)
                    for k in range(U):
                        dve.wait_ge(cand_ready[k], i + (NB * l + U))
                        dve.wait_ge(max_done, i + (U + NB * l + k))
                        dve.tensor_tensor(accm[:], accm[:], cand[:, k, :], ALU.max).then_inc(max_done, 1)
                dve.wait_ge(maxT_psum, l + 1)
                link(dve.tensor_reduce(vm[:], Xb[0].rearrange("p (b n) -> p b n", b=NB), AX.X, ALU.max))
                link(dve.tensor_tensor(vm[:], vm[:], uc[:], ALU.add))
                link(dve.scalar_tensor_tensor(mc[:], vm[:], SLOPE, vm[:], ALU.mult, ALU.max))
                link(dve.tensor_tensor(ac[:], uc[:], mc[:], ALU.subtract))
                signal(split(ac[:], [a3[:, :, k] for k in range(PARTS)], NB), a3_ready, l + 1)
                dve.wait_ge(wB_ready, 2 * l + 2)
                for c in range(NCH):
                    t0 = NB * (NCH * l + c)
                    with dve.Fori(0, NB - U + 1, U) as i:
                        for k in range(U):
                            dve.wait_ge(x_ready, i + (t0 + k + 1))
                            dve.wait_ge(p_ready, i + (t0 + k + 1))
                            dve.scalar_tensor_tensor(tmp[:, k % 2, :], wB[:, c * CH:(c + 1) * CH],
                                                     v8[:, bass.ds(i + k, 1)], X[k % 2][:],
                                                     ALU.max, ALU.add).then_inc(tmp_ready, 1)
                    n = NCH * l + c
                    dve.wait_ge(p_free, U + NB * (n + 1))
                    av4 = ACC[:, 0:2 * BANK].rearrange("p (k n) -> p k n", k=2)[:, :, 0:4 * (F + 1)] \
                        .rearrange("p k (s f) -> p k s f", f=F + 1)
                    link(dve.reciprocal(rec[:, 0:CB].rearrange("p (k s) -> p k s", k=2), av4[:, :, :, F]))
                    for k in range(2):
                        ins = dve.tensor_tensor(o[:, 4 * k:4 * k + 4, :], av4[:, k, :, 0:F],
                                                bcast(rec[:, 4 * k:4 * k + 4]), ALU.mult)
                    ins.then_inc(acc_free, 1)
                    dve.wait_ge(acc_free, n + 1)
                    dve.tensor_scalar(g[:], o[:], 0.0, None, ALU.min).then_inc(neg_ready, 1)
                    dve.wait_ge(eo_ready, n + 1)
                    link(dve.scalar_tensor_tensor(g[:], g[:], -1.0, o[:], ALU.add, ALU.max))
                    b = slice(CB * c, CB * (c + 1))
                    if l < 2:
                        link(dve.tensor_tensor(x[:, b, :], x[:, b, :], g[:], ALU.add))
                        layernorm(c).then_inc(h_ready, 1)
                    else:
                        link(dve.tensor_scalar(g[:], g[:], 1 - SLOPE, None, ALU.mult))
                        dve.scalar_tensor_tensor(h1[:, b, :], h0[:, b, :], SLOPE, g[:], ALU.mult,
                                                 ALU.add).then_inc(h_ready, 1)
                    dve.wait_ge(h_ready, NCH * (l + 1) + c + 1)

            link(dve.tensor_tensor(x[:], x[:], mb[:].unsqueeze(1).broadcast_to([P, NB, F]), ALU.add))
            dve.wait_ge(mlp_psum, 1)
            for par in range(2):
                ins = dve.tensor_tensor(x[:, par::2, :], x[:, par::2, :],
                                        X[par][:, 0:BANK].rearrange("p (b f) -> p b f", f=F), ALU.add)
                if par:
                    ins.then_inc(acc_free, 1)
                else:
                    link(ins)
            dve.wait_ge(acc_free, NCH * GAT + 1)
            for c in range(NCH):
                b = slice(CB * c, CB * (c + 1))
                link(layernorm(c))
                normalise(h0[:, b, :], h0[:, b, :], False, 1.0, 1e-24, ALU.max, g[:]).then_inc(h_ready, 1)
                dve.wait_ge(h_ready, NCH * (GAT + 1) + c + 1)

            def features(buf, src, b):
                link(dve.tensor_copy(HY[buf][:, b, 0:F], src))
                return dve.tensor_tensor(HY[buf][:, b, F:2 * F], src, HY[buf][:, b, 0:F], ALU.subtract)

            allb = slice(0, NB)
            link(dve.tensor_scalar(y[:], h0[:], HS, None, ALU.mult))
            link(features(0, y[:], allb))
            dve.wait_ge(kq_psum, 1)
            for par in range(2):
                mk = (MISC, ACC)[par][:, 0:NB * EMB].rearrange("p (b e) -> p b e", e=2 * EMB)
                link(dve.tensor_scalar(kq[:, par::2, 0:EMB], mk[:, :, 0:EMB], 1.0 / math.sqrt(EMB), None, ALU.mult))
                link(dve.tensor_copy(kq[:, par::2, EMB:], mk[:, :, EMB:]))
            link(dve.tensor_copy(kqr[:], kq[:]))
            dve.memset(Kst[:, :, KR:KR + PARTS], 0.0)
            dve.memset(Qst[:, :, KR:KR + PARTS], 1.0)
            link(dve.memset(HY[0][:, :, 2 * F:2 * F + 1], 1.0))
            Ks = Kst[:, :, 0:KR].rearrange("p n (a b e) -> p n a b e", a=PARTS, b=PARTS)
            Qs = Qst[:, :, 0:KR].rearrange("p n (a b e) -> p n a b e", a=PARTS, b=PARTS)
            for t in range(PARTS):
                link(dve.tensor_copy(Ks[:, :, 0, t, :], kqr[:, :, 0:EMB]))
                link(dve.tensor_copy(Qs[:, :, t, 0, :], kqr[:, :, EMB:]))
                if t < PARTS - 1:
                    link(dve.tensor_tensor(kqr[:, :, 0:EMB], kqr[:, :, 0:EMB], Ks[:, :, 0, t, :], ALU.subtract))
                    link(dve.tensor_tensor(kqr[:, :, EMB:], kqr[:, :, EMB:], Qs[:, :, t, 0, :], ALU.subtract))
            for t in range(1, PARTS):
                dve.tensor_copy(Ks[:, :, t, :, :], Ks[:, :, 0, :, :])
                link(dve.tensor_copy(Qs[:, :, :, t, :], Qs[:, :, :, 0, :]))
            dve.memset(accf, -BIG).then_inc(kq_ready, 1)
            dve.wait_ge(kq_ready, 1)
            tg = GAT * NCH * NB
            for c in range(NCH):
                cols = slice(c * CH, (c + 1) * CH)
                with dve.Fori(0, NB - U + 1, U) as i:
                    for k in range(U):
                        dve.wait_ge(x_ready, i + (tg + NB * c + k + 1))
                        dve.wait_ge(max_done, i + (U + NB * GAT + NB * c + k))
                        dve.tensor_tensor(accf[:, cols], accf[:, cols], X[k % 2][:], ALU.max).then_inc(max_done, 1)
            dve.wait_ge(maxT_psum, GAT + 1)
            for k in range(2):
                link(dve.tensor_reduce(vm[:, CB * k:CB * (k + 1)], X[k][:].rearrange("p (b n) -> p b n", b=CB),
                                       AX.X, ALU.max))
            link(dve.tensor_scalar(mc[:], vm[:], -1.0, None, ALU.mult))
            signal(split(mc[:], [Kst[:, :, KR + k] for k in range(PARTS)], NB), kq_ready, 2)
            for c in range(NCH):
                cols = slice(c * CH, (c + 1) * CH)
                with dve.Fori(0, NB - U + 1, U) as i:
                    for k in range(U):
                        dve.wait_ge(p_ready, i + (tg + NB * c + k + 3))
                        dve.tensor_tensor(plo[:, bass.ds(i + k, 1), cols].rearrange("p a n -> p (a n)"),
                                          e32[:, k, :],
                                          phi[:, bass.ds(i + k, 1), cols].rearrange("p a n -> p (a n)"),
                                          ALU.subtract).then_inc(lo_ready, 1)
                dve.wait_ge(p_free, U + tg + NB * (c + 1))
                for k in range(3):
                    b = slice(CB * c + TB * k, CB * c + min(TB * (k + 1), CB))
                    nb = b.stop - b.start
                    sums = ACC[:, k * BANK:k * BANK + nb * (2 * F + 1)].rearrange("p (b f) -> p b f", b=nb)
                    link(dve.reciprocal(rec[:, b], sums[:, :, 2 * F]))
                    link(dve.tensor_copy(y[:, b, :], sums[:, :, 0:F]))
                    link(dve.tensor_tensor(y[:, b, :], y[:, b, :], sums[:, :, F:2 * F], ALU.add))
                    ins = dve.tensor_tensor(y[:, b, :], y[:, b, :], bcast(rec[:, b]), ALU.mult)
                    if k < 2:
                        link(ins)
                signal(ins, acc_free, NCH * GAT + 2 + c)
                b = slice(CB * c, CB * (c + 1))
                dve.tensor_copy(res[:, b, :], y[:, b, :])
                features(1, y[:, b, :], b).then_inc(y_ready, 1)
            for q in range(3):
                for ic in range(4):
                    b = slice(4 * ic, 4 * ic + 4)
                    dve.wait_ge(f_ready, 4 * q + ic + 1)
                    link(dve.tensor_tensor(y[:, b, :], ACC[:, (ic % 2) * BANK:(ic % 2) * BANK + 4 * F]
                                           .rearrange("p (b f) -> p b f", f=F), bcast(rec[:, b]), ALU.mult))
                    if q != 1:
                        link(dve.scalar_tensor_tensor(res[:, b, :], y[:, b, :], (0.5, 0, 1.0 / 6.0)[q],
                                                      res[:, b, :], ALU.mult, ALU.add))
                    if q < 2:
                        features(q % 2, y[:, b, :], b).then_inc(y_ready, 1)
                    else:
                        dve.scalar_tensor_tensor(x[:, b, :], res[:, b, :], 1.0 / HS, x[:, b, :], ALU.mult,
                                                 ALU.add).then_inc(out_ready, 1)


def kernel(**inputs):
    import numpy as np
    import concourse.bacc as bacc
    from concourse.bass_utils import run_bass_kernel_spmd

    a = {k: np.asarray(v) for k, v in inputs.items()}
    w = np.stack([a["L0_gnn_W"], a["L1_gnn_W"], a["L2_gnn_W"][0], a["L2_gnn_W"][1]])
    arrays = {
        "x": a["x"],
        "adjT": a["adj"].T,
        "w": np.stack([w, w.transpose(0, 2, 1)]),
        "a01": np.stack([a["L0_gnn_a"].reshape(2, F).T, a["L1_gnn_a"].reshape(2, F).T]),
        "lwT": a["L2_gnn_lin_w"].transpose(0, 2, 1),
        "lb": a["L2_gnn_lin_b"].T,
        "attn": a["L2_gnn_attn"][:, :, 0].T,
        "mlp_w": a["L2_gnn_mlp_w"],
        "mlp_b": a["L2_gnn_mlp_b"].reshape(1, F),
        "wkq": np.stack([a["L3_gnn_w_k"], a["L3_gnn_w_q"]]),
        "ident": np.eye(P, dtype=np.float32),
    }
    arrays = {"in_" + k: np.ascontiguousarray(v) for k, v in arrays.items()}
    nc = bacc.Bacc("TRN2", target_bir_lowering=False, num_devices=1)
    aps = [nc.dram_tensor(k, v.shape, mybir.dt.from_np(v.dtype), kind="ExternalInput").ap()
           for k, v in arrays.items()]
    out = nc.dram_tensor("out", (N, F), mybir.dt.float32, kind="ExternalOutput").ap()
    program(nc, *aps, out)
    r = run_bass_kernel_spmd(nc, [arrays], core_ids=[0])
    return r.results[0]["out"]
```

```python
import math
from contextlib import ExitStack

import concourse.bass as bass
from concourse import mybir


P = 128
N = 2048
F = 64
NB = N // P
CH = 1024
NCH = N // CH
CB = CH // P
BANK = 512
U = 4
GAT = 4
EMB = 8
BIG = 2.0 ** 100
SLOPE = 0.2
PARTS = 3
KR = PARTS * PARTS * EMB
HS = 64.0
PS = 12 * math.log(2.0)
TB = 3


def program(nc, x_d, adjT_d, w_d, a01_d, lwT_d, lb_d, at_d, mw_d, mb_d, wkq_d, id_d, out_d):
    f32, bf16, f16, i32 = mybir.dt.float32, mybir.dt.bfloat16, mybir.dt.float16, mybir.dt.int32
    ALU, ACT, AX = mybir.AluOpType, mybir.ActivationFunctionType, mybir.AxisListType
    ctx = ExitStack()
    with ctx:
        def sb(name, shape, dt):
            return ctx.enter_context(nc.sbuf_tensor(name, shape, dt))

        def ps(name, shape):
            return ctx.enter_context(nc.psum_tensor(name, shape, f32))

        def sem(name):
            return ctx.enter_context(nc.semaphore(name))

        nadj = sb("nadj", [P, NB, N], bf16)
        phi = nadj[:].bitcast(f16)
        big = sb("big", [P, NB * N], bf16)
        plo = big[:].bitcast(f16).rearrange("p (b n) -> p b n", b=NB)
        stage = big[:, 0:4 * 2 * N].bitcast(i32).rearrange("p (s n) -> p s n", s=4)
        wide = big[:, 8 * N:8 * N + U * N].rearrange("p (u n) -> p u n", u=U)
        cand = big[:, 8 * N:8 * N + U * N].rearrange("p (u n) -> p u n", u=2 * U)
        tmp = big[:, 12 * N:14 * N].bitcast(f32).rearrange("p (u n) -> p u n", u=2)
        prob = sb("prob", [P, U, CH], f32)
        e32 = prob
        accm = sb("accm", [P, N], bf16)
        accf = big[:, 8 * N:10 * N].bitcast(f32)
        wB = sb("wB", [P, N], f32)
        KT = sb("KT", [P, N], bf16)
        QT = sb("QT", [P, N], bf16)
        rowW = KT[0:PARTS, :]
        rowA = QT[0:PARTS, :]
        ident = sb("ident", [P, P], f32)
        identb = sb("identb", [P, P], bf16)
        bigI = sb("bigI", [P, P], bf16)
        fold = sb("fold", [P, F], f32)
        ones3 = sb("ones3", [P, P], bf16)
        x = sb("x", [P, NB, F], f32)
        h0 = sb("h0", [P, NB, F], f32)
        h1 = sb("h1", [P, NB, F], f32)
        hT = [sb(f"hT{k}", [P, NB // 2 * P], f32) for k in range(3)]
        WhA = sb("WhA", [P, NB, F + 1], f32)
        wt = sb("wt", [P, GAT, F + 2], f32)
        wTt = sb("wTt", [F, GAT, P], f32)
        av = sb("av", [F, GAT, 2], f32)
        lwT = sb("lwT", [32, 2, P], f32)
        atv = sb("atv", [32, 2], f32)
        lbv = sb("lbv", [32, 2], f32)
        cb = sb("cb", [P, 2], f32)
        mw = sb("mw", [P, 3, F], f32)
        mb = sb("mb", [P, F], f32)
        wkq = sb("wkq", [P, 2 * EMB], f32)
        uv = sb("uv", [P, NB, 2], f32)
        uc = sb("uc", [P, NB], f32)
        wc = sb("wc", [P, NB], f32)
        r1 = sb("r1", [P, NB], f32)
        r2 = sb("r2", [P, NB], f32)
        v8 = sb("v8", [P, NB], f32)
        v2 = sb("v2", [P, NB], f32)
        vc = sb("vc", [P, NB], f32)
        vm = sb("vm", [P, NB], f32)
        mc = sb("mc", [P, NB], f32)
        ac = sb("ac", [P, NB], f32)
        w3 = sb("w3", [P, NB, PARTS], bf16)
        a3 = sb("a3", [P, NB, PARTS], bf16)
        rec = sb("rec", [P, NB], f32)
        o = sb("o", [P, CB, F], f32)
        g = sb("g", [P, CB, F], f32)
        s1 = sb("s1", [P, CB], f32)
        var = sb("var", [P, CB], f32)
        rstd = sb("rstd", [P, CB], f32)
        mhalf = sb("mhalf", [P, CB], f32)
        pbias = sb("pbias", [P, 1], f32)
        seed = sb("seed", [P, 5], f32)
        zeros = sb("zeros", [P, P], bf16)
        kq = sb("kq", [P, NB, 2 * EMB], f32)
        kqr = sb("kqr", [P, NB, 2 * EMB], f32)
        Kst = accm[:, 0:NB * (KR + PARTS)].rearrange("p (b r) -> p b r", b=NB)
        Qst = hT[2][:].bitcast(bf16)[:, 0:NB * (KR + PARTS)].rearrange("p (b r) -> p b r", b=NB)
        HY = [t.bitcast(f16)[:, 0:NB * (2 * F + 1)].rearrange("p (b f) -> p b f", b=NB)
              for t in (wB[:, 0:NB * (F + 1)], WhA[:].rearrange("p b f -> p (b f)"))]
        y = hT[1][:].rearrange("p (b f) -> p b f", f=F)
        res = h1
        Tsb = prob[:, 0:2, :].rearrange("p u n -> p (u n)")

        X = [ps(f"X{k}", [P, CH]) for k in range(2)]
        ACC = ps("ACC", [P, 3 * BANK])
        MISC = ps("MISC", [P, BANK])
        Rb = ACC[:, 0:2 * BANK].bitcast(bf16)
        accs = [[ACC[:, 0:BANK], ACC[:, BANK:2 * BANK]], [ACC[:, 2 * BANK:3 * BANK], MISC[:]]]
        maxT = MISC[:].bitcast(bf16)
        Ab = ACC[:, 2 * BANK:3 * BANK].bitcast(bf16)
        Xb = [t[:].bitcast(bf16) for t in X]

        def wh_bank(l, c, par):
            return ACC[:, par * BANK:(par + 1) * BANK] if l and c == 0 else X[par][:, c * BANK:(c + 1) * BANK]

        def wh_view(l, c, par):
            return wh_bank(l, c, par)[:, 0:4 * (F + 2)].rearrange("p (s f) -> p s f", f=F + 2)

        def blocks_of(c, par):
            return slice(CB * c + par, CB * (c + 1), 2)

        ld_w = sem("ld_w")
        ld_adj = [sem(f"ld_adj{k}") for k in range(4)]
        st_out = sem("st_out")
        adj_ready = sem("adj_ready")
        consts = sem("consts")
        dve_const = sem("dve_const")
        dve_step = sem("dve_step")
        pe_prep = sem("pe_prep")
        prep_ready = sem("prep_ready")
        h_ready = sem("h_ready")
        hT_psum = sem("hT_psum")
        hT_ready = sem("hT_ready")
        wh_psum = sem("wh_psum")
        v_ready = sem("v_ready")
        hT_early_psum = sem("hT_early_psum")
        hT_early_ready = sem("hT_early_ready")
        wh_early_psum = sem("wh_early_psum")
        v_early_ready = sem("v_early_ready")
        wh_ready = sem("wh_ready")
        w3_ready = sem("w3_ready")
        wrow_psum = sem("wrow_psum")
        wrow_ready = sem("wrow_ready")
        wB_psum = sem("wB_psum")
        wB_ready = sem("wB_ready")
        cand_ready = [sem(f"cand_ready{k}") for k in range(U)]
        max_done = sem("max_done")
        accm_clear = sem("accm_clear")
        maxT_psum = sem("maxT_psum")
        a3_ready = sem("a3_ready")
        arow_psum = sem("arow_psum")
        arow_ready = sem("arow_ready")
        x_ready = sem("x_ready")
        tmp_ready = sem("tmp_ready")
        p_ready = sem("p_ready")
        lo_ready = sem("lo_ready")
        p_free = sem("p_free")
        neg_ready = sem("neg_ready")
        eo_ready = sem("eo_ready")
        acc_free = sem("acc_free")
        var_ready = sem("var_ready")
        rstd_ready = sem("rstd_ready")
        mlp_psum = sem("mlp_psum")
        kq_psum = sem("kq_psum")
        kq_ready = sem("kq_ready")
        kqT_psum = sem("kqT_psum")
        kqT_ready = sem("kqT_ready")
        t_ready = sem("t_ready")
        t_sb = sem("t_sb")
        f_ready = sem("f_ready")
        y_ready = sem("y_ready")
        out_ready = sem("out_ready")

        block = ctx.enter_context(nc.Block())

        def max_base(l):
            return 2 * U + (NB * (2 * l - 1) if l else 0)

        def cand_base(l):
            return NB * (2 * l - 1) if l else 0

        EARLY = NCH * NB - 2 * U
        N_C = 8
        N_W = 20

        @block.sync
        def _(sp):
            xv = x_d.rearrange("(b p) f -> p b f", p=P)
            sp.dma_start(x[:], xv).then_inc(ld_w, 16)
            sp.dma_start(ident[:], id_d).then_inc(ld_w, 16)
            for half in range(2):
                lo = half * F
                sp.dma_start(wt[lo:lo + F, :, 0:F], w_d[0].rearrange("l k f -> k l f")).then_inc(ld_w, 16)
                sp.dma_start(wTt[:, :, lo:lo + F], w_d[1].rearrange("l k f -> k l f")).then_inc(ld_w, 16)
                sp.dma_start(mw[lo:lo + F, :, :], mw_d.rearrange("(t c) f -> c t f", c=F)).then_inc(ld_w, 16)
                sp.dma_start(wkq[lo:lo + F, 0:EMB], wkq_d[0]).then_inc(ld_w, 16)
                sp.dma_start(wkq[lo:lo + F, EMB:2 * EMB], wkq_d[1]).then_inc(ld_w, 16)
                sp.dma_start(fold[lo:lo + F, :], id_d[0:F, 0:F]).then_inc(ld_w, 16)
            sp.dma_start(lwT[:], lwT_d.rearrange("l h c -> h l c")).then_inc(ld_w, 16)
            sp.dma_start(atv[:], at_d).then_inc(ld_w, 16)
            sp.dma_start(lbv[:], lb_d).then_inc(ld_w, 16)
            sp.dma_start(mb[:], mb_d.broadcast_to([P, F])).then_inc(ld_w, 16)
            for l in range(2):
                sp.dma_start(av[:, l, :], a01_d[l]).then_inc(ld_w, 16)
            for s in range(4):
                sp.dma_start(stage[:, s, :], adjT_d[s * P:(s + 1) * P, :]).then_inc(ld_adj[s], 16)
            with sp.Fori(4, NB - 3, 4) as i:
                for s in range(4):
                    sp.wait_ge(adj_ready, i + (s - 3))
                    sp.dma_start(stage[:, s, :],
                                 adjT_d[bass.ds((i + s) * P, P), :]).then_inc(ld_adj[s], 16)
            ov = out_d.rearrange("(b p) f -> p b f", p=P)
            for c in range(4):
                sp.wait_ge(out_ready, c + 1)
                sp.dma_start(ov[:, 4 * c:4 * c + 4, :], x[:, 4 * c:4 * c + 4, :]).then_inc(st_out, 16)
            sp.wait_ge(st_out, 64)

        @block.gpsimd
        def _(pool):
            pool.memset(ones3[:], 0.0).then_inc(consts, 1)
            pool.memset(KT[:], 0.0).then_inc(consts, 1)
            pool.memset(zeros[:], 0.0).then_inc(consts, 1)
            pool.memset(QT[:], 0.0).then_inc(consts, 1)
            pool.wait_ge(consts, 1)
            pool.memset(ones3[0:PARTS, :], 1.0).then_inc(consts, 1)
            pool.memset(pbias[:], PS).then_inc(consts, 1)
            pool.memset(WhA[:, :, F:F + 1], 1.0).then_inc(consts, 1)
            pool.memset(mhalf[:], -0.5).then_inc(consts, 1)
            n_rstd = [0]

            def inverse_root():
                n_rstd[0] += 1
                pool.wait_ge(var_ready, n_rstd[0])
                pool.tensor_tensor(rstd[:], var[:], mhalf[:], ALU.pow).then_inc(rstd_ready, 1)

            for c in range(NCH):
                if c == 0:
                    pool.wait_ge(consts, N_C)
                inverse_root()
            def start_maxima(l):
                if l:
                    pool.wait_ge(maxT_psum, NCH * l)
                pool.memset(accm[:], -BIG).then_inc(accm_clear, 1)

            def candidates(l, first, end):
                for s in range(first, end):
                    k, jb = s % U, s % NB
                    if k < 2:
                        continue
                    if l == 0:
                        pool.wait_ge(adj_ready, jb + 1)
                        pool.wait_ge(max_done, s + U + 1)
                        dst, src = wide[:, k, :], nadj[:, jb, :]
                    else:
                        pool.wait_ge(max_done, max_base(l) + s - 2 * U + 1)
                        c = s // NB
                        dst, src = cand[:, s % (2 * U), :], nadj[:, jb, c * CH:(c + 1) * CH]
                    pool.tensor_scalar(dst, src, BIG, vc[:, jb:jb + 1], ALU.mult, ALU.add).then_inc(cand_ready[k], U)

            start_maxima(0)
            for l in range(GAT):
                pool.wait_ge(v_ready, l + 1)
                candidates(l, CB if l else 0, NCH * NB if l else NB)
                if l < 2:
                    inverse_root()
                if l < GAT - 1:
                    start_maxima(l + 1)
                    pool.wait_ge(v_early_ready, l + 1)
                    candidates(l + 1, 0, CB)
                if l < 2:
                    inverse_root()
            for c in range(2 * NCH):
                inverse_root()

        @block.scalar
        def _(act):
            act.wait_ge(consts, N_C)

            def candidate(l, c, i, k):
                act.wait_ge(max_done, i + (max_base(l) + NB * c + k - 2 * U + 1))
                src = nadj[:, bass.ds(i + k, 1), c * CH:(c + 1) * CH].rearrange("p a n -> p (a n)")
                act.activation(cand[:, k % (2 * U), :], src, ACT.Identity, bias=vc[:, bass.ds(i + k, 1)],
                               scale=BIG).then_inc(cand_ready[k % U], U)

            def w_rows(l):
                act.wait_ge(wrow_psum, l + 1)
                act.activation(rowW, Rb[0:PARTS, :], ACT.Copy).then_inc(wrow_ready, 1)

            def row_copy(l, c):
                act.wait_ge(arow_psum, NCH * l + c + 1)
                act.activation(rowA[:, c * CH:(c + 1) * CH], Ab[0:PARTS, :], ACT.Copy).then_inc(arow_ready, 1)

            def exponential(l, c, i, k):
                t0 = NB * (NCH * l + c)
                act.wait_ge(tmp_ready, i + (t0 + k + 3))
                act.wait_ge(p_free, i + (t0 + k + 1))
                act.activation(prob[:, k % U, :], tmp[:, k % 2, :], ACT.Exp,
                               bias=v2[:, bass.ds(i + k, 1)]).then_inc(p_ready, 1)

            for l in range(GAT):
                slot = (0, 0, 0, 1)[l]
                act.wait_ge(hT_psum, l + 1)
                new = slice(BANK if l else 0, CH)
                act.activation(hT[slot][:, new], X[0][:, new], ACT.Copy).then_inc(hT_ready, 1)
                for c in range(NCH):
                    if l == 0 or c:
                        act.wait_ge(v_ready, l + 1)
                    for par in range(2):
                        ins = act.activation(WhA[:, blocks_of(c, par), 0:F], wh_view(l, c, par)[:, :, 0:F], ACT.Copy)
                        if c:
                            ins.then_inc(wh_ready, 1)
                if l == 0:
                    w_rows(l)
                if l == 0:
                    with act.Fori(0, NB - U + 1, U) as i:
                        for k in range(2):
                            act.wait_ge(adj_ready, i + (k + 1))
                            act.wait_ge(max_done, i + (U + k + 1))
                            act.activation(wide[:, k, :],
                                           nadj[:, bass.ds(i + k, 1), :].rearrange("p a n -> p (a n)"),
                                           ACT.Identity, bias=vc[:, bass.ds(i + k, 1)],
                                           scale=BIG).then_inc(cand_ready[k], U)
                else:
                    for k in range(2 * U, NB):
                        if k % U < 2:
                            candidate(l, 0, 0, k)
                        if k == 2 * U + 1:
                            w_rows(l)
                for k in range(2):
                    act.wait_ge(wB_psum, 2 * l + k + 1)
                    act.activation(wB[:, k * CH:(k + 1) * CH], X[k][:], ACT.Copy).then_inc(wB_ready, 1)
                if l:
                    for k in (0, 1, U, U + 1):
                        candidate(l, 1, 0, k)
                row_copy(l, 0)
                if l == 0:
                    row_copy(l, 1)
                if l:
                    for k in range(2):
                        candidate(l, 1, 0, 2 * U + k)
                for k in range(2 * U):
                    exponential(l, 0, 0, k)
                    if l and k in (2, 3):
                        candidate(l, 1, 0, 2 * U + k + 2)
                for k in range(2 * U, 3 * U):
                    exponential(l, 0, 0, k)
                if l:
                    row_copy(l, 1)
                for k in range(3 * U, 4 * U):
                    exponential(l, 0, 0, k)
                for k in range(U):
                    exponential(l, 1, 0, k)
                act.wait_ge(neg_ready, NCH * l + 1)
                act.activation(g[:], g[:], ACT.Exp).then_inc(eo_ready, 1)
                with act.Fori(U, NB - 2 * U + 1, U) as i:
                    for k in range(U):
                        exponential(l, 1, i, k)
                for k in range(3 * U, 4 * U):
                    exponential(l, 1, 0, k)
                    if l < GAT - 1 and k == NB - 3:
                        act.wait_ge(hT_early_psum, l + 1)
                        act.activation(hT[(0, 0, 1)[l]][:, 0:BANK], ACC[:, 0:BANK],
                                       ACT.Copy).then_inc(hT_early_ready, 1)
                if l < GAT - 1:
                    act.wait_ge(v_early_ready, l + 1)
                    for k in range(2):
                        candidate(l + 1, 0, 0, k)
                act.wait_ge(neg_ready, NCH * l + 2)
                act.activation(g[:], g[:], ACT.Exp).then_inc(eo_ready, 1)
                if l < GAT - 1:
                    for k in (U, U + 1):
                        candidate(l + 1, 0, 0, k)
                if l == GAT - 1:
                    act.wait_ge(hT_psum, GAT + 1)
                    act.activation(hT[2][:], X[0][:], ACT.Copy).then_inc(hT_ready, 1)
            act.wait_ge(hT_psum, GAT + 2)
            act.activation(hT[0][:], X[0][:], ACT.Copy).then_inc(hT_ready, 1)
            act.wait_ge(kqT_psum, 1)
            act.activation(KT[0:KR + PARTS, :], Xb[0][0:KR + PARTS, :], ACT.Copy)
            act.activation(QT[0:KR + PARTS, :], Xb[1][0:KR + PARTS, :], ACT.Copy).then_inc(kqT_ready, 1)
            act.wait_ge(kqT_psum, 2)
            act.activation(KT[0:KR + PARTS, :], Xb[0][0:KR + PARTS, :], ACT.Copy).then_inc(kqT_ready, 1)
            tg = GAT * NCH * NB
            tm = NCH * NB
            for c in range(NCH):
                with act.Fori(0, NB - U + 1, U) as i:
                    for k in range(U):
                        t = tg + NB * c + k
                        act.wait_ge(x_ready, i + (tm + t + 1))
                        act.wait_ge(lo_ready, i + (NB * c + k + 1))
                        act.activation(e32[:, k, :], X[k % 2][:], ACT.Exp, bias=pbias[:, 0:1])
                        act.activation(phi[:, bass.ds(i + k, 1), c * CH:(c + 1) * CH]
                                       .rearrange("p a n -> p (a n)"),
                                       X[k % 2][:], ACT.Exp, bias=pbias[:, 0:1]).then_inc(p_ready, 1)
            for q in range(3):
                for ic in range(4):
                    act.wait_ge(t_ready, 4 * q + ic + 1)
                    act.activation(Tsb[:, ic * BANK:(ic + 1) * BANK],
                                   X[ic // 2][:, (ic % 2) * BANK:(ic % 2 + 1) * BANK],
                                   ACT.Copy).then_inc(t_sb, 1)

        @block.tensor
        def _(pe):
            def transpose_h(src, chunks, prior, dst, done):
                for c in chunks:
                    pe.wait_ge(h_ready, prior + c + 1)
                    for k in range(4 * c, 4 * c + 4):
                        last = pe.transpose(dst[:, k * P:(k + 1) * P],
                                            src[:, 2 * k:2 * k + 2, :].rearrange("p a f -> p (a f)"), ident[:])
                last.then_inc(done, 1)

            def features(l, chunks, done):
                for c in chunks:
                    for b in range(CB * c, CB * (c + 1)):
                        at = (b // 2 % 4) * (F + 2)
                        last = pe.matmul(wh_bank(l, c, b % 2)[:, at:at + F + 2], lhs(hT[(0, 0, 0, 1)[l]], b),
                                         half(wt, b)[:, l, :], start=True, stop=True)
                last.then_inc(done, 1)

            def lhs(t, b):
                return t[F * (b % 2):F * (b % 2) + F, (b // 2) * P:(b // 2 + 1) * P]

            def half(t, b):
                return t[F * (b % 2):F * (b % 2) + F]

            pe.wait_ge(ld_w, 16 * N_W)
            for l in range(2):
                for t in range(2):
                    pe.matmul(MISC[0:F, 2 * l + t:2 * l + t + 1], lwT[:, l, t * F:(t + 1) * F],
                              atv[:, l:l + 1], start=True, stop=True)
                last = pe.matmul(MISC[:, 8 + l:9 + l], lbv[:, l:l + 1].broadcast_to([32, P]), atv[:, l:l + 1],
                                 start=True, stop=True)
            last.then_inc(pe_prep, 1)
            pe.wait_ge(prep_ready, 1)
            for l in range(GAT):
                last = pe.matmul(MISC[:, 16 + 2 * l:18 + 2 * l], wTt[:, l, :], av[:, l, :], start=True, stop=True)
            last.then_inc(pe_prep, 1)
            pe.wait_ge(prep_ready, 2)
            pe.wait_ge(dve_const, 2)

            def mask_tile(n, c, jb, row):
                buf = X[n % 2]
                pe.wait_ge(row["free"], row["count"])
                for s in range(2):
                    pe.matmul(buf[:, s * BANK:(s + 1) * BANK], bigI[:],
                              row["mask"][:, s * BANK:(s + 1) * BANK], start=True, stop=False)
                for s in range(2):
                    last = pe.matmul(buf[:, s * BANK:(s + 1) * BANK], row["lhs"],
                                     row["rhs"][:, s * BANK:(s + 1) * BANK], start=False, stop=True)
                last.then_inc(x_ready, 1)

            def mask_at(c, jb):
                return nadj[:, bass.ds(jb, 1), c * CH:(c + 1) * CH].rearrange("p a n -> p (a n)")

            def score_gat(l, c, jb, k):
                mask_tile(k, c, jb, {"free": tmp_ready, "count": jb + (NB * (NCH * l + c) + 1), "mask": mask_at(c, jb),
                                     "lhs": ones3[:], "rhs": QT[:, c * CH:(c + 1) * CH]})

            def products_gat(l, c, jb, k):
                pe.wait_ge(p_ready, jb + (NB * (NCH * l + c) + 3))
                rhs = WhA[:, bass.ds(jb, 1), :].rearrange("p a n -> p (a n)")
                for b in range(CB):
                    at = (b % 4) * (F + 1)
                    last = pe.matmul(accs[c][b // 4][:, at:at + F + 1], prob[:, k % U, b * P:(b + 1) * P], rhs,
                                     start=False, stop=False, skip_group_check=True)
                last.then_inc(p_free, 1)

            def clear(l, c):
                for bank in accs[c]:
                    for at in range(0, 4 * (F + 1), P):
                        n = min(P, 4 * (F + 1) - at)
                        pe.matmul(bank[:, at:at + n], zeros[:], identb[:, 0:n], start=at == 0, stop=False,
                                  skip_group_check=True)

            def max_rows(l, c):
                for b in range(CB):
                    n = CB * c + b
                    last = pe.transpose(maxT[:, b * P:(b + 1) * P], accm[:, n * P:(n + 1) * P], identb[:])
                last.then_inc(maxT_psum, 1)

            def a_rows(l, c):
                pe.wait_ge(a3_ready, NCH * l + c + 1)
                for b in range(CB):
                    last = pe.transpose(Ab[0:PARTS, b * P:(b + 1) * P], a3[:, CB * c + b, :], identb[:])
                last.then_inc(arow_psum, 1)

            for l in range(GAT):
                rest = (1,) if l else (0, 1)
                transpose_h((h0, h0, h0, h1)[l], rest, NCH * l, X[0], hT_psum)
                pe.wait_ge(hT_ready, l + 1)
                features(l, rest, wh_psum)
                pe.wait_ge(w3_ready, l + 1)
                pe.wait_ge(wh_ready, 2 * l + 2)
                for b in range(NB):
                    last = pe.transpose(Rb[0:PARTS, b * P:(b + 1) * P], w3[:, b, :], identb[:])
                last.then_inc(wrow_psum, 1)
                pe.wait_ge(wrow_ready, l + 1)
                for k in range(2):
                    for s in range(2):
                        at = k * CH + s * BANK
                        last = pe.matmul(X[k][:, s * BANK:(s + 1) * BANK], ones3[:], KT[:, at:at + BANK],
                                         start=True, stop=True)
                    last.then_inc(wB_psum, 1)
                pe.wait_ge(wB_ready, 2 * l + 2)
                pe.wait_ge(max_done, max_base(l) + NB)
                max_rows(l, 0)
                a_rows(l, 0)
                if l == 0:
                    max_rows(l, 1)
                    pe.wait_ge(arow_ready, 1)
                    a_rows(l, 1)
                pe.wait_ge(arow_ready, NCH * l + (2 if l == 0 else 1))
                clear(l, 0)
                score_gat(l, 0, 0, 0)
                score_gat(l, 0, 1, 1)
                with pe.Fori(0, U + 1, U) as i:
                    for k in range(U):
                        score_gat(l, 0, i + (k + 2), k)
                        products_gat(l, 0, i + k, k)
                if l:
                    pe.wait_ge(max_done, max_base(l) + NCH * NB)
                    max_rows(l, 1)
                for k in range(2 * U, NB):
                    if k == NB - U and l:
                        a_rows(l, 1)
                    if k == NB - 2:
                        pe.wait_ge(arow_ready, NCH * l + 2)
                        clear(l, 1)
                    if k < NB - 2:
                        score_gat(l, 0, k + 2, k)
                    else:
                        score_gat(l, 1, k + 2 - NB, k)
                    products_gat(l, 0, k, k)
                with pe.Fori(0, NB - 2 * U + 1, U) as i:
                    for k in range(U):
                        score_gat(l, 1, i + (k + 2), k)
                        products_gat(l, 1, i + k, k)
                for k in range(NB - U, NB):
                    if k < NB - 2:
                        score_gat(l, 1, k + 2, k)
                    if l < GAT - 1 and k == NB - 3:
                        transpose_h((h0, h0, h1)[l], (0,), NCH * (l + 1), ACC, hT_early_psum)
                    if l < GAT - 1 and k == NB - 1:
                        pe.wait_ge(hT_early_ready, l + 1)
                        features(l + 1, (0,), wh_early_psum)
                    products_gat(l, 1, k, k)

            transpose_h(h1, (0, 1), NCH * GAT, X[0], hT_psum)
            pe.wait_ge(hT_ready, GAT + 1)
            pe.wait_ge(acc_free, NCH * GAT)
            for b in range(NB):
                out = X[b % 2][:, (b // 2) * F:(b // 2 + 1) * F]
                for t in range(3):
                    last = pe.matmul(out, lhs(hT[t], b), half(mw, b)[:, t, :], start=t == 0, stop=t == 2)
            last.then_inc(mlp_psum, 1)

            transpose_h(h0, (0, 1), NCH * (GAT + 1), X[0], hT_psum)
            pe.wait_ge(hT_ready, GAT + 2)
            for b in range(NB):
                last = pe.matmul((MISC, ACC)[b % 2][:, (b // 2) * 2 * EMB:(b // 2 + 1) * 2 * EMB], lhs(hT[0], b), half(wkq, b),
                                 start=True, stop=True)
            last.then_inc(kq_psum, 1)
            pe.wait_ge(kq_ready, 1)
            for b in range(NB):
                pe.transpose(Xb[0][0:KR + PARTS, b * P:(b + 1) * P], Kst[:, b, :], identb[:])
                last = pe.transpose(Xb[1][0:KR + PARTS, b * P:(b + 1) * P], Qst[:, b, :], identb[:])
            last.then_inc(kqT_psum, 1)
            pe.wait_ge(kqT_ready, 1)

            def score_taylor(free, n0, c, jb, k):
                mask_tile(k, c, jb, {"free": free, "count": jb + n0, "mask": mask_at(c, jb),
                                     "lhs": QT[:, bass.ds(jb * P, P)],
                                     "rhs": KT[:, c * CH:(c + 1) * CH]})

            for c in range(NCH):
                with pe.Fori(0, NB - U + 1, U) as i:
                    for k in range(U):
                        score_taylor(max_done, max_base(GAT) + NB * c - 1, c, i + k, k)
            pe.wait_ge(max_done, max_base(GAT) + NCH * NB)
            for b in range(NB):
                last = pe.transpose(X[b // CB][:, (b % CB) * P:(b % CB + 1) * P], accf[:, b * P:(b + 1) * P], ident[:])
            last.then_inc(maxT_psum, 1)
            pe.wait_ge(kq_ready, 2)
            for b in range(NB):
                last = pe.transpose(Xb[0][0:KR + PARTS, b * P:(b + 1) * P], Kst[:, b, :], identb[:])
            last.then_inc(kqT_psum, 1)
            pe.wait_ge(kqT_ready, 2)

            def products_taylor(c, jb, first, last_tile):
                n = GAT * NCH * NB + NB * c
                pe.wait_ge(p_ready, jb + (n + 3))
                pe.wait_ge(lo_ready, jb + (U + NB * c + 1))
                rhs = HY[0][:, bass.ds(jb, 1), :].rearrange("p a n -> p (a n)")
                for b in range(CB):
                    at = (b // TB) * BANK + (b % TB) * (2 * F + 1)
                    cols = slice(c * CH + b * P, c * CH + (b + 1) * P)
                    for part in (phi, plo):
                        last = pe.matmul(ACC[:, at:at + 2 * F + 1],
                                         part[:, bass.ds(jb, 1), cols].rearrange("p a n -> p (a n)"), rhs,
                                         start=first and b % TB == 0 and part is phi, stop=last_tile and part is plo,
                                         skip_group_check=True)
                last.then_inc(p_free, 1)

            for c in range(NCH):
                n0 = NB * (NCH * GAT + c) + 1
                score_taylor(p_ready, n0, c, 0, 0)
                score_taylor(p_ready, n0, c, 1, 1)
                if c:
                    pe.wait_ge(acc_free, NCH * GAT + 1 + c)
                else:
                    pe.wait_ge(acc_free, NCH * GAT + 1)
                for k in range(NB):
                    if k < NB - 2:
                        score_taylor(p_ready, n0, c, k + 2, k)
                    products_taylor(c, k, k == 0, k == NB - 1)

            def turn_back(q, ic):
                pe.wait_ge(t_sb, 4 * q + ic + 1)
                before = 4 * q + ic - 2
                if before < 8:
                    pe.wait_ge(y_ready, NCH + max(before + 1, 0))
                else:
                    pe.wait_ge(out_ready, before - 7)
                for b in range(4):
                    last = pe.matmul(ACC[:, (ic % 2) * BANK + b * F:(ic % 2) * BANK + (b + 1) * F],
                                     Tsb[:, ic * BANK + b * P:ic * BANK + (b + 1) * P], fold[:],
                                     start=True, stop=True)
                last.then_inc(f_ready, 1)

            for q in range(3):
                for ic in range(4):
                    out = X[ic // 2][:, (ic % 2) * BANK:(ic % 2 + 1) * BANK]
                    if q:
                        pe.wait_ge(t_sb, 4 * (q - 1) + ic + 1)
                    cols = slice(ic * BANK, (ic + 1) * BANK)

                    def pair(jb, first, final):
                        lhsT = HY[(q + 1) % 2][:, bass.ds(jb, 1), 0:2 * F].rearrange("p a n -> p (a n)")
                        pe.matmul(out, lhsT, phi[:, bass.ds(jb, 1), cols].rearrange("p a n -> p (a n)"),
                                  start=first, stop=False)
                        return pe.matmul(out, lhsT, plo[:, bass.ds(jb, 1), cols].rearrange("p a n -> p (a n)"),
                                         start=False, stop=final)

                    for jb4 in range(4):
                        if ic == 0:
                            pe.wait_ge(y_ready, (NCH * (jb4 // 2) // 2 + 1) if q == 0 else NCH + 4 * (q - 1) + jb4 + 1)
                        for jb in range(4 * jb4, 4 * jb4 + 4):
                            if jb == NB - 1 and ic:
                                turn_back(q, ic - 1)
                            last = pair(jb, jb == 0, jb == NB - 1)
                    last.then_inc(t_ready, 1)
                turn_back(q, 3)

        @block.vector
        def _(dve):
            steps = [0]

            def link(ins):
                steps[0] += 1
                ins.then_inc(dve_step, 1)
                dve.wait_ge(dve_step, steps[0])

            def signal(ins, s, value):
                ins.then_inc(s, 1)
                dve.wait_ge(s, value)

            def bcast(t, n=F):
                return t.unsqueeze(2).broadcast_to([P, t.shape[1], n])

            n_rstd = [0]

            def normalise(src, dst, relu, var_scale, eps, mode, scratch):
                link(dve.tensor_reduce(s1[:], src, AX.X, ALU.add))
                link(dve.tensor_scalar(s1[:], s1[:], 1.0 / F, None, ALU.mult))
                yield
                link(dve.tensor_tensor(scratch, src, bcast(s1[:]), ALU.subtract))
                link(dve.tensor_tensor(o[:], scratch, scratch, ALU.mult))
                yield
                link(dve.tensor_reduce(s1[:], o[:], AX.X, ALU.add))
                dve.tensor_scalar(var[:], s1[:], var_scale, eps, ALU.mult, mode).then_inc(var_ready, 1)
                n_rstd[0] += 1
                count = n_rstd[0]
                yield
                yield
                dve.wait_ge(rstd_ready, count)
                if relu:
                    return dve.scalar_tensor_tensor(dst, scratch, 0.0, bcast(rstd[:]), ALU.max, ALU.mult)
                return dve.tensor_tensor(dst, scratch, bcast(rstd[:]), ALU.mult)

            def layernorm(c):
                b = slice(CB * c, CB * (c + 1))
                return run(normalise(x[:, b, :], h0[:, b, :], True, 1.0 / F, 1e-5, ALU.add, g[:]))

            def split(src, dst, n):
                link(dve.tensor_copy(dst[0], src))
                link(dve.tensor_tensor(r1[:, 0:n], src, dst[0], ALU.subtract))
                link(dve.tensor_copy(dst[1], r1[:, 0:n]))
                link(dve.tensor_tensor(r2[:, 0:n], r1[:, 0:n], dst[1], ALU.subtract))
                return dve.tensor_copy(dst[2], r2[:, 0:n])

            def max_step(l, c, i, k):
                s0 = NB * c + k
                dve.wait_ge(cand_ready[k % U], i + (cand_base(l) + NB * c + k - k % U + U))
                dve.wait_ge(max_done, i + (max_base(l) + s0))
                cols = slice(c * CH, (c + 1) * CH)
                dve.tensor_tensor(accm[:, cols], accm[:, cols], cand[:, k % (2 * U), :], ALU.max).then_inc(max_done, 1)

            def source_terms(l, chunks, done):
                for c in chunks:
                    for par in range(2):
                        ins = dve.tensor_copy(uv[:, blocks_of(c, par), :], wh_view(l, c, par)[:, :, F:F + 2])
                link(ins)
                b = slice(CB * chunks[0], CB * (chunks[-1] + 1))
                dve.tensor_copy(vc[:, b], uv[:, b, 1]).then_inc(done, 1)

            def target_terms(l, c):
                b = slice(CB * c, CB * (c + 1))
                dve.wait_ge(maxT_psum, NCH * l + c + 1)
                link(dve.tensor_reduce(vm[:, b], maxT.rearrange("p (b n) -> p b n", b=CB), AX.X, ALU.max))
                link(dve.tensor_tensor(vm[:, b], vm[:, b], uc[:, b], ALU.add))
                link(dve.scalar_tensor_tensor(mc[:, b], vm[:, b], SLOPE, vm[:, b], ALU.mult, ALU.max))
                link(dve.tensor_tensor(ac[:, b], uc[:, b], mc[:, b], ALU.subtract))
                signal(split(ac[:, b], [a3[:, b, k] for k in range(PARTS)], CB), a3_ready, NCH * l + c + 1)

            def exponents(l, c, i, k):
                t0 = NB * (NCH * l + c)
                dve.wait_ge(x_ready, i + (t0 + k + 1))
                dve.wait_ge(p_ready, i + (t0 + k + 1))
                dve.scalar_tensor_tensor(tmp[:, k % 2, :], wB[:, c * CH:(c + 1) * CH], v8[:, bass.ds(i + k, 1)],
                                         X[k % 2][:], ALU.max, ALU.add).then_inc(tmp_ready, 1)

            def outputs(l, c):
                n = NCH * l + c
                dve.wait_ge(p_free, U + NB * (n + 1))
                sums = [bank[:, 0:4 * (F + 1)].rearrange("p (s f) -> p s f", f=F + 1) for bank in accs[c]]
                for k in range(2):
                    ins = dve.reciprocal(rec[:, 4 * k:4 * k + 4], sums[k][:, :, F])
                link(ins)
                for k in range(2):
                    ins = dve.tensor_tensor(o[:, 4 * k:4 * k + 4, :], sums[k][:, :, 0:F],
                                            bcast(rec[:, 4 * k:4 * k + 4]), ALU.mult)
                signal(ins, acc_free, n + 1)
                dve.tensor_scalar(g[:], o[:], 0.0, None, ALU.min).then_inc(neg_ready, 1)
                yield
                yield
                dve.wait_ge(eo_ready, n + 1)
                link(dve.scalar_tensor_tensor(g[:], g[:], -1.0, o[:], ALU.add, ALU.max))
                b = slice(CB * c, CB * (c + 1))
                if l < 2:
                    link(dve.tensor_tensor(x[:, b, :], x[:, b, :], g[:], ALU.add))
                    yield
                    ins = yield from normalise(x[:, b, :], h0[:, b, :], True, 1.0 / F, 1e-5, ALU.add, g[:])
                    ins.then_inc(h_ready, 1)
                else:
                    link(dve.tensor_scalar(g[:], g[:], 1 - SLOPE, None, ALU.mult))
                    dve.scalar_tensor_tensor(h1[:, b, :], h0[:, b, :], SLOPE, g[:], ALU.mult,
                                             ALU.add).then_inc(h_ready, 1)
                dve.wait_ge(h_ready, NCH * (l + 1) + c + 1)

            def run(work):
                while True:
                    try:
                        next(work)
                    except StopIteration as end:
                        return end.value

            dve.wait_ge(ld_w, 16 * N_W)
            dve.wait_ge(consts, N_C)
            for n, (start, count) in enumerate([(tmp_ready, 2), (p_ready, 2), (max_done, 2 * U), (p_free, U), (lo_ready, U)]):
                dve.memset(seed[:, n:n + 1], 0.0).then_inc(start, count)
            dve.tensor_copy(identb[:], ident[:]).then_inc(dve_const, 1)
            dve.tensor_scalar(bigI[:], ident[:], BIG, None, ALU.mult).then_inc(dve_const, 1)
            dve.wait_ge(pe_prep, 1)
            dve.tensor_copy(cb[:], MISC[:, 8:10])
            dve.tensor_copy(av[:, 2:4, :], MISC[0:F, 0:4].rearrange("p (l t) -> p l t", l=2)).then_inc(prep_ready, 1)
            for c in range(NCH):
                layernorm(c).then_inc(h_ready, 1)
                dve.wait_ge(h_ready, c + 1)
            dve.wait_ge(pe_prep, 2)
            dve.tensor_copy(wt[:, :, F:F + 2],
                            MISC[:, 16:16 + 2 * GAT].rearrange("p (l t) -> p l t", l=GAT)).then_inc(prep_ready, 1)

            for l in range(GAT):
                dve.wait_ge(wh_psum, l + 1)
                source_terms(l, (1,) if l else (0, 1), v_ready)
                dve.tensor_scalar(v8[:], uv[:, :, 1], 1 - SLOPE, None, ALU.mult)
                dve.tensor_scalar(v2[:], uv[:, :, 1], SLOPE, None, ALU.mult)
                if l >= 2:
                    link(dve.tensor_scalar(uc[:], uv[:, :, 0], cb[:, l - 2:l - 1], None, ALU.add))
                else:
                    link(dve.tensor_copy(uc[:], uv[:, :, 0]))
                link(dve.tensor_scalar(wc[:], uc[:], -(1 - SLOPE), None, ALU.mult))
                signal(split(wc[:], [w3[:, :, k] for k in range(PARTS)], NB), w3_ready, l + 1)
                if l == 0:
                    dve.wait_ge(accm_clear, 1)
                    with dve.Fori(0, NB - U + 1, U) as i:
                        for k in range(U):
                            dve.wait_ge(ld_adj[k], i * 4 + 16)
                            dve.tensor_scalar(nadj[:, bass.ds(i + k, 1), :].rearrange("p a n -> p (a n)"),
                                              stage[:, k, :], 0, -1.0, ALU.is_gt, ALU.add).then_inc(adj_ready, 1)
                        for k in range(U):
                            dve.wait_ge(cand_ready[k], i + U)
                            dve.wait_ge(max_done, i + (2 * U + k))
                            dve.tensor_tensor(accm[:], accm[:], wide[:, k, :], ALU.max).then_inc(max_done, 1)
                else:
                    for k in range(2 * U, NB):
                        max_step(l, 0, 0, k)
                target_terms(l, 0)
                if l == 0:
                    target_terms(l, 1)
                else:
                    for k in range(U):
                        max_step(l, 1, 0, k)
                dve.wait_ge(wB_ready, 2 * l + 2)
                for k in range(2 * U):
                    exponents(l, 0, 0, k)
                    if l:
                        for step in (U + 2 * k, U + 2 * k + 1) if k < U else (2 * U + k,):
                            max_step(l, 1, 0, step)
                for k in range(2 * U, 3 * U):
                    exponents(l, 0, 0, k)
                    if l and k == 2 * U + 1:
                        target_terms(l, 1)
                for k in range(3 * U, 4 * U):
                    exponents(l, 0, 0, k)
                for k in range(U):
                    exponents(l, 1, 0, k)
                work = outputs(l, 0)
                for k in range(U, NB - U):
                    next(work, None)
                    exponents(l, 1, 0, k)
                for _ in work:
                    pass
                for k in range(3 * U, 4 * U):
                    exponents(l, 1, 0, k)
                if l < GAT - 1:
                    dve.wait_ge(wh_early_psum, l + 1)
                    source_terms(l + 1, (0,), v_early_ready)
                    dve.wait_ge(accm_clear, l + 2)
                    for k in range(2):
                        max_step(l + 1, 0, 0, k)
                run(outputs(l, 1))
                if l < GAT - 1:
                    for k in range(2, 2 * U):
                        max_step(l + 1, 0, 0, k)

            link(dve.tensor_tensor(x[:], x[:], mb[:].unsqueeze(1).broadcast_to([P, NB, F]), ALU.add))
            dve.wait_ge(mlp_psum, 1)
            for par in range(2):
                ins = dve.tensor_tensor(x[:, par::2, :], x[:, par::2, :],
                                        X[par][:, 0:BANK].rearrange("p (b f) -> p b f", f=F), ALU.add)
                if par:
                    ins.then_inc(acc_free, 1)
                else:
                    link(ins)
            dve.wait_ge(acc_free, NCH * GAT + 1)
            for c in range(NCH):
                b = slice(CB * c, CB * (c + 1))
                link(layernorm(c))
                run(normalise(h0[:, b, :], h0[:, b, :], False, 1.0, 1e-24, ALU.max, g[:])).then_inc(h_ready, 1)
                dve.wait_ge(h_ready, NCH * (GAT + 1) + c + 1)

            def features(buf, src, b):
                link(dve.tensor_copy(HY[buf][:, b, 0:F], src))
                return dve.tensor_tensor(HY[buf][:, b, F:2 * F], src, HY[buf][:, b, 0:F], ALU.subtract)

            allb = slice(0, NB)
            link(dve.tensor_scalar(y[:], h0[:], HS, None, ALU.mult))
            link(features(0, y[:], allb))
            dve.wait_ge(kq_psum, 1)
            for par in range(2):
                mk = (MISC, ACC)[par][:, 0:NB * EMB].rearrange("p (b e) -> p b e", e=2 * EMB)
                link(dve.tensor_scalar(kq[:, par::2, 0:EMB], mk[:, :, 0:EMB], 1.0 / math.sqrt(EMB), None, ALU.mult))
                link(dve.tensor_copy(kq[:, par::2, EMB:], mk[:, :, EMB:]))
            link(dve.tensor_copy(kqr[:], kq[:]))
            dve.memset(Kst[:, :, KR:KR + PARTS], 0.0)
            dve.memset(Qst[:, :, KR:KR + PARTS], 1.0)
            link(dve.memset(HY[0][:, :, 2 * F:2 * F + 1], 1.0))
            Ks = Kst[:, :, 0:KR].rearrange("p n (a b e) -> p n a b e", a=PARTS, b=PARTS)
            Qs = Qst[:, :, 0:KR].rearrange("p n (a b e) -> p n a b e", a=PARTS, b=PARTS)
            for t in range(PARTS):
                link(dve.tensor_copy(Ks[:, :, 0, t, :], kqr[:, :, 0:EMB]))
                link(dve.tensor_copy(Qs[:, :, t, 0, :], kqr[:, :, EMB:]))
                if t < PARTS - 1:
                    link(dve.tensor_tensor(kqr[:, :, 0:EMB], kqr[:, :, 0:EMB], Ks[:, :, 0, t, :], ALU.subtract))
                    link(dve.tensor_tensor(kqr[:, :, EMB:], kqr[:, :, EMB:], Qs[:, :, t, 0, :], ALU.subtract))
            for t in range(1, PARTS):
                dve.tensor_copy(Ks[:, :, t, :, :], Ks[:, :, 0, :, :])
                link(dve.tensor_copy(Qs[:, :, :, t, :], Qs[:, :, :, 0, :]))
            dve.memset(accf, -BIG).then_inc(kq_ready, 1)
            dve.wait_ge(kq_ready, 1)
            tg = GAT * NCH * NB
            for c in range(NCH):
                cols = slice(c * CH, (c + 1) * CH)
                with dve.Fori(0, NB - U + 1, U) as i:
                    for k in range(U):
                        dve.wait_ge(x_ready, i + (tg + NB * c + k + 1))
                        dve.wait_ge(max_done, i + (max_base(GAT) + NB * c + k))
                        dve.tensor_tensor(accf[:, cols], accf[:, cols], X[k % 2][:], ALU.max).then_inc(max_done, 1)
            dve.wait_ge(maxT_psum, NCH * GAT + 1)
            for k in range(2):
                link(dve.tensor_reduce(vm[:, CB * k:CB * (k + 1)], X[k][:].rearrange("p (b n) -> p b n", b=CB),
                                       AX.X, ALU.max))
            link(dve.tensor_scalar(mc[:], vm[:], -1.0, None, ALU.mult))
            signal(split(mc[:], [Kst[:, :, KR + k] for k in range(PARTS)], NB), kq_ready, 2)
            for c in range(NCH):
                cols = slice(c * CH, (c + 1) * CH)
                with dve.Fori(0, NB - U + 1, U) as i:
                    for k in range(U):
                        dve.wait_ge(p_ready, i + (tg + NB * c + k + 3))
                        dve.tensor_tensor(plo[:, bass.ds(i + k, 1), cols].rearrange("p a n -> p (a n)"),
                                          e32[:, k, :],
                                          phi[:, bass.ds(i + k, 1), cols].rearrange("p a n -> p (a n)"),
                                          ALU.subtract).then_inc(lo_ready, 1)
                dve.wait_ge(p_free, U + tg + NB * (c + 1))
                for k in range(3):
                    b = slice(CB * c + TB * k, CB * c + min(TB * (k + 1), CB))
                    nb = b.stop - b.start
                    sums = ACC[:, k * BANK:k * BANK + nb * (2 * F + 1)].rearrange("p (b f) -> p b f", b=nb)
                    link(dve.reciprocal(rec[:, b], sums[:, :, 2 * F]))
                    link(dve.tensor_copy(y[:, b, :], sums[:, :, 0:F]))
                    link(dve.tensor_tensor(y[:, b, :], y[:, b, :], sums[:, :, F:2 * F], ALU.add))
                    ins = dve.tensor_tensor(y[:, b, :], y[:, b, :], bcast(rec[:, b]), ALU.mult)
                    if k < 2:
                        link(ins)
                signal(ins, acc_free, NCH * GAT + 2 + c)
                b = slice(CB * c, CB * (c + 1))
                dve.tensor_copy(res[:, b, :], y[:, b, :])
                features(1, y[:, b, :], b).then_inc(y_ready, 1)
            for q in range(3):
                for ic in range(4):
                    b = slice(4 * ic, 4 * ic + 4)
                    dve.wait_ge(f_ready, 4 * q + ic + 1)
                    link(dve.tensor_tensor(y[:, b, :], ACC[:, (ic % 2) * BANK:(ic % 2) * BANK + 4 * F]
                                           .rearrange("p (b f) -> p b f", f=F), bcast(rec[:, b]), ALU.mult))
                    if q != 1:
                        link(dve.scalar_tensor_tensor(res[:, b, :], y[:, b, :], (0.5, 0, 1.0 / 6.0)[q],
                                                      res[:, b, :], ALU.mult, ALU.add))
                    if q < 2:
                        features(q % 2, y[:, b, :], b).then_inc(y_ready, 1)
                    else:
                        dve.scalar_tensor_tensor(x[:, b, :], res[:, b, :], 1.0 / HS, x[:, b, :], ALU.mult,
                                                 ALU.add).then_inc(out_ready, 1)


def kernel(**inputs):
    import numpy as np
    import concourse.bacc as bacc
    from concourse.bass_utils import run_bass_kernel_spmd

    a = {k: np.asarray(v) for k, v in inputs.items()}
    w = np.stack([a["L0_gnn_W"], a["L1_gnn_W"], a["L2_gnn_W"][0], a["L2_gnn_W"][1]])
    arrays = {
        "x": a["x"],
        "adjT": a["adj"].T,
        "w": np.stack([w, w.transpose(0, 2, 1)]),
        "a01": np.stack([a["L0_gnn_a"].reshape(2, F).T, a["L1_gnn_a"].reshape(2, F).T]),
        "lwT": a["L2_gnn_lin_w"].transpose(0, 2, 1),
        "lb": a["L2_gnn_lin_b"].T,
        "attn": a["L2_gnn_attn"][:, :, 0].T,
        "mlp_w": a["L2_gnn_mlp_w"],
        "mlp_b": a["L2_gnn_mlp_b"].reshape(1, F),
        "wkq": np.stack([a["L3_gnn_w_k"], a["L3_gnn_w_q"]]),
        "ident": np.eye(P, dtype=np.float32),
    }
    arrays = {"in_" + k: np.ascontiguousarray(v) for k, v in arrays.items()}
    nc = bacc.Bacc("TRN2", target_bir_lowering=False, num_devices=1)
    aps = [nc.dram_tensor(k, v.shape, mybir.dt.from_np(v.dtype), kind="ExternalInput").ap()
           for k, v in arrays.items()]
    out = nc.dram_tensor("out", (N, F), mybir.dt.float32, kind="ExternalOutput").ap()
    program(nc, *aps, out)
    r = run_bass_kernel_spmd(nc, [arrays], core_ids=[0])
    return r.results[0]["out"]
```
